# Optimizing a Trainium2 kernel written in Bass

```python
import numpy as np
import jax
import jax.numpy as jnp

def _softmax(x, axis=-1):
    return jax.nn.softmax(x, axis=axis)

def _gelu(x):
    return jax.nn.gelu(x, approximate=True)

def _silu(x):
    return jax.nn.silu(x)

def _sigmoid(x):
    return jax.nn.sigmoid(x)

def _layernorm(x, axis=-1, eps=1e-05):
    m = jnp.mean(x, axis=axis, keepdims=True)
    v = jnp.var(x, axis=axis, keepdims=True)
    return (x - m) / jnp.sqrt(v + eps)

def _scatter_add(tgt, idx, src, axis=0):
    return tgt.at[idx].add(src)

def _segment_sum(src, seg, n):
    return jax.ops.segment_sum(src, seg, n)
kernel_name = 'mk_adj_resnorm_d2_adj_r2_5c1b46'

def setup_inputs(seed: int=0):
    np.random.seed(seed)
    _w = jnp.asarray

    def _rec_inputs():
        import jax
        import jax.numpy as jnp
        _gk = jax.random.key(seed)
        x = -0.0001538 + 1 * jax.random.normal(jax.random.fold_in(_gk, 1), (128, 128, 384), jnp.float32)
        _a = jax.random.bernoulli(jax.random.fold_in(_gk, 2), 0.03125, (128, 128, 128))
        _a = jnp.logical_or(_a, jnp.eye(128, dtype=bool))
        adj = _a
        return (x, adj)
    x, adj = _rec_inputs()

    def _L0_gnn_setup():
        import jax, jax.numpy as jnp
        import numpy as np
        B, S, H = (4, 1024, 384)
        NUM_HEADS = 6
        HEAD_SIZE = H // NUM_HEADS
        NEG = -9000000000000000.0

        def _heads(x):
            b, s, _ = x.shape
            return x.reshape(b, s, NUM_HEADS, HEAD_SIZE).transpose(0, 2, 1, 3)
        key = jax.random.key(seed)
        ks = jax.random.split(key, 10)
        seq_inputs = jax.random.normal(ks[0], (B, S, H), dtype=jnp.float32)
        gm = jax.random.randint(ks[1], (B, S, S), 0, 2) > 0
        graph_mask = gm | jnp.eye(S, dtype=bool)[None]
        sc = 1.0 / np.sqrt(H)
        Wq = jax.random.normal(ks[2], (H, H), dtype=jnp.float32) * sc
        bq = jnp.zeros((H,), dtype=jnp.float32)
        Wk = jax.random.normal(ks[3], (H, H), dtype=jnp.float32) * sc
        bk = jnp.zeros((H,), dtype=jnp.float32)
        Wv = jax.random.normal(ks[4], (H, H), dtype=jnp.float32) * sc
        bv = jnp.zeros((H,), dtype=jnp.float32)
        Wf = jax.random.normal(ks[5], (H, H), dtype=jnp.float32) * sc
        bf = jnp.zeros((H,), dtype=jnp.float32)
        return {'seq_inputs': seq_inputs, 'Wq': Wq, 'bq': bq, 'Wk': Wk, 'bk': bk, 'Wv': Wv, 'bv': bv, 'Wf': Wf, 'bf': bf, 'graph_mask': graph_mask}
    _L0_gnn_all = _L0_gnn_setup()
    _L0_gnn_in = {k: v for k, v in _L0_gnn_all.items() if k in ('Wq', 'bq', 'Wk', 'bk', 'Wv', 'bv', 'Wf', 'bf')}
    del _L0_gnn_all

    def _L1_gnn_setup():
        import jax, jax.numpy as jnp
        import numpy as np
        ATT_HEAD = 12
        IN_DIM = 384
        OUT_DIM = IN_DIM // ATT_HEAD
        LEAKY_ALPHA = 0.2
        B, N = (8, 256)
        key = jax.random.key(seed)
        ks = jax.random.split(key, 8)
        feat_in = jax.random.normal(ks[0], (B, N, IN_DIM), dtype=jnp.float32)
        adj = jax.random.randint(ks[1], (B, N, N), 0, 2) > 0
        lim_W = float(np.sqrt(6.0 / (IN_DIM + OUT_DIM)))
        W = jax.random.uniform(ks[2], (ATT_HEAD, IN_DIM, OUT_DIM), minval=-lim_W, maxval=lim_W, dtype=jnp.float32)
        b = jnp.zeros((OUT_DIM,), dtype=jnp.float32)
        lim_w = float(np.sqrt(6.0 / (OUT_DIM + 1)))
        w_src = jax.random.uniform(ks[3], (ATT_HEAD, OUT_DIM, 1), minval=-lim_w, maxval=lim_w, dtype=jnp.float32)
        w_dst = jax.random.uniform(ks[4], (ATT_HEAD, OUT_DIM, 1), minval=-lim_w, maxval=lim_w, dtype=jnp.float32)
        std_H = float(np.sqrt(2.0 / (IN_DIM + IN_DIM)))
        H_w = jax.random.normal(ks[5], (IN_DIM, IN_DIM), dtype=jnp.float32) * std_H
        H_b = jax.random.normal(ks[6], (IN_DIM,), dtype=jnp.float32) * 0.01
        return {'feat_in': feat_in, 'adj': adj, 'W': W, 'b': b, 'w_src': w_src, 'w_dst': w_dst, 'H_w': H_w, 'H_b': H_b}
    _L1_gnn_all = _L1_gnn_setup()
    _L1_gnn_in = {k: v for k, v in _L1_gnn_all.items() if k in ('W', 'b', 'w_src', 'w_dst', 'H_w', 'H_b')}
    del _L1_gnn_all
    return {'x': x, 'adj': adj, 'L0_gnn_Wq': _L0_gnn_in['Wq'], 'L0_gnn_bq': _L0_gnn_in['bq'], 'L0_gnn_Wk': _L0_gnn_in['Wk'], 'L0_gnn_bk': _L0_gnn_in['bk'], 'L0_gnn_Wv': _L0_gnn_in['Wv'], 'L0_gnn_bv': _L0_gnn_in['bv'], 'L0_gnn_Wf': _L0_gnn_in['Wf'], 'L0_gnn_bf': _L0_gnn_in['bf'], 'L1_gnn_W': _L1_gnn_in['W'], 'L1_gnn_b': _L1_gnn_in['b'], 'L1_gnn_w_src': _L1_gnn_in['w_src'], 'L1_gnn_w_dst': _L1_gnn_in['w_dst'], 'L1_gnn_H_w': _L1_gnn_in['H_w'], 'L1_gnn_H_b': _L1_gnn_in['H_b']}

def reference(x, adj, L0_gnn_Wq, L0_gnn_bq, L0_gnn_Wk, L0_gnn_bk, L0_gnn_Wv, L0_gnn_bv, L0_gnn_Wf, L0_gnn_bf, L1_gnn_W, L1_gnn_b, L1_gnn_w_src, L1_gnn_w_dst, L1_gnn_H_w, L1_gnn_H_b):
    import jax
    import jax.numpy as jnp

    def _L0_gnn_ref(seq_inputs, Wq, bq, Wk, bk, Wv, bv, Wf, bf, graph_mask):
        import jax, jax.numpy as jnp
        import numpy as np
        B, S, H = (4, 1024, 384)
        NUM_HEADS = 6
        HEAD_SIZE = H // NUM_HEADS
        NEG = -9000000000000000.0

        def _heads(x):
            b, s, _ = x.shape
            return x.reshape(b, s, NUM_HEADS, HEAD_SIZE).transpose(0, 2, 1, 3)
        q = _heads(seq_inputs @ Wq + bq)
        k = _heads(seq_inputs @ Wk + bk)
        v = _heads(seq_inputs @ Wv + bv)
        scores = jnp.einsum('bhqd,bhkd->bhqk', q, k) / np.sqrt(HEAD_SIZE)
        bias = jnp.where(graph_mask, 0.0, NEG)[:, None]
        probs = jax.nn.softmax(scores + bias, axis=-1)
        ctx = jnp.einsum('bhqk,bhkd->bhqd', probs, v)
        ctx = ctx.transpose(0, 2, 1, 3).reshape(seq_inputs.shape[0], seq_inputs.shape[1], H)
        return ctx @ Wf + bf

    def _L1_gnn_ref(feat_in, adj, W, b, w_src, w_dst, H_w, H_b):
        import jax, jax.numpy as jnp
        import numpy as np
        ATT_HEAD = 12
        IN_DIM = 384
        OUT_DIM = IN_DIM // ATT_HEAD
        LEAKY_ALPHA = 0.2
        B, N = (8, 256)
        h = jnp.einsum('bnd,ade->bane', feat_in, W)
        th = jnp.tanh(h)
        attn_src = jnp.einsum('bane,aeo->bano', th, w_src)
        attn_dst = jnp.einsum('bane,aeo->bano', th, w_dst)
        attn = attn_src + jnp.swapaxes(attn_dst, 2, 3)
        attn = jnp.where(attn >= 0, attn, LEAKY_ALPHA * attn)
        mask = ~adj[:, None, :, :]
        attn = jnp.where(mask, jnp.float32(-999.0), attn)
        attn = jax.nn.softmax(attn, axis=-1)
        feat_out = jnp.einsum('banm,bame->bane', attn, h) + b
        feat_out = jnp.swapaxes(feat_out, 1, 2).reshape(feat_in.shape[0], feat_in.shape[1], -1)
        feat_out = jax.nn.elu(feat_out)
        gate = jax.nn.sigmoid(feat_in @ H_w.T + H_b)
        return gate * feat_out + (1.0 - gate) * feat_in
    x = _layernorm(x + _L0_gnn_ref(x, L0_gnn_Wq, L0_gnn_bq, L0_gnn_Wk, L0_gnn_bk, L0_gnn_Wv, L0_gnn_bv, L0_gnn_Wf, L0_gnn_bf, adj), axis=-1)
    x = _layernorm(x + _L1_gnn_ref(x, adj, L1_gnn_W, L1_gnn_b, L1_gnn_w_src, L1_gnn_w_dst, L1_gnn_H_w, L1_gnn_H_b), axis=-1)
    return x

_drawn_inputs = setup_inputs


def setup_inputs(seed=0):
    import zlib

    import numpy as np

    out = dict(_drawn_inputs(seed))
    spreads = {'L0_gnn_bq': (0.0, 0.1),
     'L0_gnn_bk': (0.0, 2.0),
     'L0_gnn_bv': (0.0, 0.1),
     'L0_gnn_bf': (0.0, 0.1),
     'L1_gnn_b': (0.0, 0.1)}
    factors = {'L1_gnn_H_b': 33.02}
    for name, (base, spread) in spreads.items():
        noise = np.random.default_rng([zlib.crc32(name.encode()), seed]).standard_normal(out[name].shape)
        drawn = base * np.exp(spread * noise) if base else spread * noise
        out[name] = jnp.asarray(drawn.astype(out[name].dtype))
    for name, factor in factors.items():
        out[name] = (out[name] * factor).astype(out[name].dtype)
    return out
```

```python
from contextlib import ExitStack

import concourse.bass as bass
from concourse import mybir

F32 = mybir.dt.float32
F32R = mybir.dt.float32r
BF16 = mybir.dt.bfloat16
U8 = mybir.dt.uint8
ALU = mybir.AluOpType
ACT = mybir.ActivationFunctionType
AX = mybir.AxisListType

P = 128
PAIR = 2
HEADS0 = 6
HEADS1 = 12
PARTS = 3
MASKED = -9.0e15
EPS = 1e-5
SLOPE = 0.2

RING = 5
JOBS = [
    ("xT0", "A"), ("xT1", "A"), ("ctx0", "B"), ("ctx1", "B"), ("qk0", "A"),
    ("out0", "B"), ("out1", "B"), ("qk1", "A"), ("agg0", "C"), ("qk2", "A"),
    ("x1T0", "B"), ("x1T1", "B"), ("v0", "A"), ("v1", "A"), ("agg1", "C"),
    ("h0", "B"), ("g0", "B"), ("h1", "B"), ("g1", "B"), ("s00", "A"),
    ("s01", "A"), ("s10", "A"), ("s11", "A"), ("thT0", "B"), ("thT1", "B"),
    ("sd", "B"), ("pT00", "A"), ("pT01", "A"), ("pT10", "A"), ("pT11", "A"),
]
SLOT = {name: k for k, (name, _) in enumerate(JOBS)}
LOGIT_JOBS = [("aT0", "C"), ("aT1", "C"), ("z0", "B"), ("z1", "B")]
LAG = {"A": 0, "B": 1, "C": 2}


def tenant_before(jobs, name, tick, pairs):
    at = [n for n, _ in jobs].index(name)
    if pairs is None:
        n, stage = jobs[at - 1]
        return n, tick - LAG[stage] - (at == 0)
    earlier = [(tick, job) for job in jobs[:at]]
    for back in range(1, 4):
        earlier = [(tick - back, job) for job in jobs] + earlier
    for at_tick, (n, stage) in reversed(earlier):
        if 0 <= at_tick - LAG[stage] < pairs:
            return n, at_tick - LAG[stage]
    return None


def build(nc, x, adj, weights, bias_rows, bias_cols, w_sd, ident, ident_h, pick_s, pick_d, out):
    B, _, D = x.shape
    C = D // P
    DH0 = D // HEADS0
    DH1 = D // HEADS1
    AUG = DH1 + 1
    NP = B // PAIR
    G0 = HEADS0 // 2
    G1 = 4
    NZ = HEADS1 // G1
    SD = 2 * HEADS1
    ROWS = PARTS * SD
    Q_SCALE = float(DH0) ** -0.5
    WQ, WK, WV, WF, WH, WG = range(6)
    BV, BF, BH, BG = range(4)
    assert NP > 4 and C * P == D

    with ExitStack() as ctx:
        def sb(name, shape, dt=F32):
            return ctx.enter_context(nc.sbuf_tensor(name, shape, dt))

        def sem(name):
            return ctx.enter_context(nc.semaphore(name))

        ring = [ctx.enter_context(nc.psum_tensor(f"ring{k}", [P, 512], F32)) for k in range(RING)]
        logit = [ctx.enter_context(nc.psum_tensor(f"logit{k}", [P, 512], F32)) for k in range(NZ)]

        w_f32 = sb("w_f32", [P, C, D])
        w_hi = sb("w_hi", [P, 6, C, D], F32R)
        w_lo = sb("w_lo", [P, 6, C, D], F32R)
        rows = sb("rows", [P, 4, D])
        cols = sb("cols", [P, 2, C])
        wsd = sb("wsd", [P, C, SD])
        idf = sb("idf", [P, P])
        idh = sb("idh", [P, P], BF16)
        picks = sb("picks", [ROWS, HEADS1, P], BF16)
        pickd = sb("pickd", [ROWS, HEADS1, P], BF16)
        neg_half = sb("neg_half", [P, 1])
        eps = sb("eps", [P, 1])
        x_in = sb("x_in", [P, PAIR, D])
        adj_in = sb("adj_in", [P, PAIR, P], U8)
        mask_a = sb("mask_a", [P, PAIR, P], BF16)
        x_res = sb("x_res", [P, PAIR, D])
        xT_hi = sb("xT_hi", [P, C, PAIR, P], F32R)
        xT_lo = sb("xT_lo", [P, C, PAIR, P], F32R)
        qT = sb("qT", [P, C, PAIR, P])
        kT = sb("kT", [P, C, PAIR, P])
        v = sb("v", [P, PAIR, D])
        neg_max = sb("neg_max", [P, PAIR, HEADS0])
        p_sum = sb("p_sum", [P, PAIR, HEADS0])
        p_inv = sb("p_inv", [P, PAIR, HEADS0])
        prob = sb("prob", [P, PAIR, HEADS0, P])
        probT = sb("probT", [P, PAIR, HEADS0, P])
        mask_b = sb("mask_b", [P, PAIR, P], BF16)
        ctxT_hi = sb("ctxT_hi", [P, PAIR, C, P], F32R)
        ctxT_lo = sb("ctxT_lo", [P, PAIR, C, P], F32R)
        y0 = sb("y0", [P, PAIR, D])
        stats0 = sb("stats0", [P, PAIR, 6])
        mv0 = sb("mv0", [P, PAIR, 2])
        ve0 = sb("ve0", [P, PAIR])
        rstd0 = sb("rstd0", [P, PAIR])
        x1 = sb("x1", [P, PAIR, D])
        x1T_hi = sb("x1T_hi", [P, PAIR, C, P], F32R)
        x1T_lo = sb("x1T_lo", [P, PAIR, C, P], F32R)
        h_aug = sb("h_aug", [P, PAIR, HEADS1, AUG])
        th = sb("th", [P, PAIR, D])
        thT = sb("thT", [P, PAIR, C, P])
        g_pre = sb("g_pre", [P, PAIR, D])
        g_tanh = sb("g_tanh", [P, PAIR, D])
        gate = sb("gate", [P, PAIR, D])
        gx = sb("gx", [P, PAIR, D])
        sd_parts = sb("sd_parts", [P, PAIR, PARTS, SD], BF16)
        sd_rest = sb("sd_rest", [P, PAIR, SD])
        sd_rest2 = sb("sd_rest2", [P, PAIR, SD])
        sdT = sb("sdT", [ROWS, PAIR, P], BF16)
        z_relu = sb("z_relu", [P, PAIR, HEADS1, P])
        att = sb("att", [P, PAIR, HEADS1, P])
        att_max = sb("att_max", [P, PAIR, HEADS1])
        attT = sb("attT", [P, PAIR, HEADS1, P])
        a_inv = sb("a_inv", [P, PAIR, HEADS1])
        f = sb("f", [P, PAIR, D])
        f_neg = sb("f_neg", [P, PAIR, D])
        f_exp = sb("f_exp", [P, PAIR, D])
        elu1 = sb("elu1", [P, PAIR, D])
        gated = sb("gated", [P, PAIR, D])
        y1 = sb("y1", [P, PAIR, D])
        stats1 = sb("stats1", [P, PAIR, 6])
        mv1 = sb("mv1", [P, PAIR, 2])
        ve1 = sb("ve1", [P, PAIR])
        rstd1 = sb("rstd1", [P, PAIR])
        y_out = sb("y_out", [P, PAIR, D])

        const_in = sem("const_in")
        w_in = sem("w_in")
        w_rounded = sem("w_rounded")
        w_split = sem("w_split")
        bq_scaled = sem("bq_scaled")
        ones_set = sem("ones_set")
        half_set = sem("half_set")
        x_loaded = sem("x_loaded")
        adj_loaded = sem("adj_loaded")
        stored = sem("stored")
        xT_made, qk_made, v_made = sem("xT_made"), sem("qk_made"), sem("v_made")
        s_made, pT_made, ctx_made = sem("s_made"), sem("pT_made"), sem("ctx_made")
        out_made, x1T_made, h_made = sem("out_made"), sem("x1T_made"), sem("h_made")
        g_made, thT_made, sd_made = sem("g_made"), sem("thT_made"), sem("sd_made")
        sdT_made, z_made, aT_made, agg_made = sem("sdT_made"), sem("z_made"), sem("aT_made"), sem("agg_made")
        xhi_set, xlo_set, q_set, k_set, v_set = (sem(n) for n in ("xhi_set", "xlo_set", "q_set", "k_set", "v_set"))
        max_set, prob_set, inv_set, norm_set, pT_set = (sem(n) for n in ("max_set", "prob_set", "inv_set", "norm_set", "pT_set"))
        chi_set, clo_set, y0_set, st0_set, mv0_set = (sem(n) for n in ("chi_set", "clo_set", "y0_set", "st0_set", "mv0_set"))
        ve0_set, rstd0_set, x1_set, x1hi_set, x1lo_set = (sem(n) for n in ("ve0_set", "rstd0_set", "x1_set", "x1hi_set", "x1lo_set"))
        h_set, th_set, thT_set, gpre_set, gtanh_set = (sem(n) for n in ("h_set", "th_set", "thT_set", "gpre_set", "gtanh_set"))
        gate_set, gx_set, part_set, sdT_set = (sem(n) for n in ("gate_set", "gx_set", "part_set", "sdT_set"))
        relu_set, leaky_set, amax_set, shift_set, att_set = (sem(n) for n in ("relu_set", "leaky_set", "amax_set", "shift_set", "att_set"))
        aT_set, ainv_set, f_set, fneg_set, fexp_set = (sem(n) for n in ("aT_set", "ainv_set", "f_set", "fneg_set", "fexp_set"))
        elu_set, gated_set, y1_set, st1_set, mv1_set = (sem(n) for n in ("elu_set", "gated_set", "y1_set", "st1_set", "mv1_set"))
        ve1_set, rstd1_set, yout_set = (sem(n) for n in ("ve1_set", "rstd1_set", "yout_set"))
        maska_set, maskb_set, xres_set = (sem(n) for n in ("maska_set", "maskb_set", "xres_set"))

        N_CONST = 7

        def need(eng, s, value):
            if not isinstance(value, int) or value > 0:
                eng.wait_ge(s, value)

        def run_ticks(eng, tick):
            def peeled(t):
                tick(t, NP, t < NP, 1 <= t < NP + 1, 2 <= t)
            for t in range(3):
                peeled(t)
            with eng.Fori(3, NP) as t:
                tick(t, None, True, True, True)
            for t in range(NP, NP + 2):
                peeled(t)

        def ring_bank(name):
            return ring[SLOT[name] % RING]

        readers = {"sd": [(sdT_set, 1, 1)]}
        for g in range(PAIR):
            readers[f"xT{g}"] = [(xlo_set, 2, g + 1)]
            readers[f"ctx{g}"] = [(clo_set, 2, g + 1)]
            readers[f"out{g}"] = [(y0_set, 2, g + 1)]
            readers[f"agg{g}"] = [(f_set, 2, g + 1)]
            readers[f"x1T{g}"] = [(x1lo_set, 2, g + 1)]
            readers[f"v{g}"] = [(v_set, 2, g + 1)]
            readers[f"h{g}"] = [(h_set, 2, g + 1)]
            readers[f"g{g}"] = [(gpre_set, 2, g + 1)]
            readers[f"thT{g}"] = [(thT_set, 2, g + 1)]
            for half in range(2):
                readers[f"s{g}{half}"] = [(prob_set, 4, 2 * g + half + 1)]
                readers[f"pT{g}{half}"] = [(pT_set, 4, 2 * g + half + 1)]
        for k in range(C):
            readers[f"qk{k}"] = [(k_set, C, k + 1)]
        logit_readers = [{f"{kind}{g}": [(s, 6, NZ * g + j + 1)] for g in range(PAIR)
                          for kind, s in (("aT", aT_set), ("z", leaky_set))} for j in range(NZ)]

        def wait_read(eng, tenant, readers):
            if tenant is not None:
                name, pair = tenant
                for s, per_pair, count in readers[name]:
                    eng.wait_ge(s, per_pair * pair + count)

        def ring_wait(eng, name, t, static):
            wait_read(eng, tenant_before(JOBS[SLOT[name] % RING::RING], name, t, static), readers)

        def logit_wait(eng, j, name, t, static):
            wait_read(eng, tenant_before(LOGIT_JOBS, name, t, static), logit_readers[j])

        block = ctx.enter_context(nc.Block())

        @block.sync
        def _(sp):
            for dst, src in ((idf[:], ident), (idh[:], ident_h), (picks[:], pick_s), (pickd[:], pick_d),
                             (rows[:], bias_rows), (cols[:], bias_cols), (wsd[:], w_sd)):
                sp.dma_start(dst, src).then_inc(const_in, 16)
            sp.dma_start(x_in[:], x[0:PAIR].rearrange("b n d -> n b d")).then_inc(x_loaded, 16)
            sp.dma_start(adj_in[:], adj[:, 0:PAIR, :]).then_inc(adj_loaded, 16)
            for n in range(6):
                need(sp, w_split, n)
                sp.dma_start(w_f32[:], weights[n]).then_inc(w_in, 16)

            def tick(t, static, a, b, c):
                following, done = (t + 1) * PAIR, (t - 2) * PAIR
                if a and (static is None or t + 1 < NP):
                    sp.wait_ge(maska_set, t + 1)
                    sp.wait_ge(xT_made, 2 * t + 2)
                    sp.wait_ge(xres_set, 2 * t + 2)
                    sp.dma_start(x_in[:], x[bass.ds(following, PAIR)].rearrange("b n d -> n b d")).then_inc(x_loaded, 16)
                    sp.dma_start(adj_in[:], adj[:, bass.ds(following, PAIR), :]).then_inc(adj_loaded, 16)
                if c:
                    sp.wait_ge(yout_set, 2 * (t - 2) + 2)
                    sp.dma_start(out[bass.ds(done, PAIR)].rearrange("b n d -> n b d"), y_out[:]).then_inc(stored, 16)

            tick(0, NP, True, False, False)
            tick(1, NP, True, True, False)
            with sp.Fori(2, NP - 1) as t:
                tick(t, None, True, True, True)
            for t in range(NP - 1, NP + 2):
                tick(t, NP, t < NP, t <= NP, True)
            sp.wait_ge(stored, 16 * NP)

        @block.tensor
        def _(pe):
            def split_product(dst, terms):
                for n, (stationary, moving) in enumerate(terms):
                    mm = pe.matmul(dst, stationary, moving, start=(n == 0), stop=(n == len(terms) - 1))
                return mm

            def rows_by_weight(name, hiT, loT, w):
                terms = []
                for k in range(C):
                    terms += [(hiT(k), w_hi[:, w, k, :]), (hiT(k), w_lo[:, w, k, :]), (loT(k), w_hi[:, w, k, :])]
                return split_product(ring_bank(name)[:, 0:D], terms)

            def tick(t, static, a, b, c):
                pa, pb, pc = t, t - 1, t - 2

                def transpose_x(g):
                    if g == 0:
                        pe.wait_ge(x_loaded, 16 * pa + 16)
                    ring_wait(pe, f"xT{g}", t, static)
                    for k in range(C):
                        mm = pe.transpose(ring_bank(f"xT{g}")[:, k * P:(k + 1) * P], x_in[:, g, k * P:(k + 1) * P], idf[:])
                    mm.then_inc(xT_made, 1)

                def context(g):
                    pe.wait_ge(pT_set, 4 * pb + 2 * g + 2)
                    ring_wait(pe, f"ctx{g}", t, static)
                    bank = ring_bank(f"ctx{g}")
                    for k in range(C):
                        for half in range(2):
                            mm = pe.matmul(bank[DH0 * half:DH0 * half + DH0, k * P:(k + 1) * P],
                                           v[:, g, (2 * k + half) * DH0:(2 * k + half + 1) * DH0],
                                           probT[:, g, half * G0 + k, :], start=True, stop=True)
                    mm.then_inc(ctx_made, 1)

                def qk(k):
                    if k == 0:
                        pe.wait_ge(xlo_set, 2 * pa + 2)
                    ring_wait(pe, f"qk{k}", t, static)
                    bank = ring_bank(f"qk{k}")
                    for n, w in enumerate((WQ, WK)):
                        terms = []
                        for j in range(C):
                            tile = slice(k * P, (k + 1) * P)
                            hi, lo = (xT[:, j, :, :].rearrange("p g n -> p (g n)") for xT in (xT_hi, xT_lo))
                            terms += [(w_hi[:, w, j, tile], hi), (w_hi[:, w, j, tile], lo), (w_lo[:, w, j, tile], hi)]
                        mm = split_product(bank[:, n * PAIR * P:(n + 1) * PAIR * P], terms)
                    mm.then_inc(qk_made, 1)

                def out_projection(g):
                    pe.wait_ge(clo_set, 2 * pb + g + 1)
                    ring_wait(pe, f"out{g}", t, static)
                    rows_by_weight(f"out{g}", lambda k: ctxT_hi[:, g, k, :], lambda k: ctxT_lo[:, g, k, :], WF)\
                        .then_inc(out_made, 1)

                def transpose_x1(g):
                    pe.wait_ge(x1_set, 2 * pb + g + 1)
                    ring_wait(pe, f"x1T{g}", t, static)
                    for k in range(C):
                        mm = pe.transpose(ring_bank(f"x1T{g}")[:, k * P:(k + 1) * P], x1[:, g, k * P:(k + 1) * P], idf[:])
                    mm.then_inc(x1T_made, 1)

                def value(g):
                    ring_wait(pe, f"v{g}", t, static)
                    rows_by_weight(f"v{g}", lambda k: xT_hi[:, k, g, :], lambda k: xT_lo[:, k, g, :], WV)\
                        .then_inc(v_made, 1)

                def hidden_and_gate(g):
                    pe.wait_ge(x1lo_set, 2 * pb + g + 1)
                    for name, w, made in ((f"h{g}", WH, h_made), (f"g{g}", WG, g_made)):
                        ring_wait(pe, name, t, static)
                        rows_by_weight(name, lambda k: x1T_hi[:, g, k, :], lambda k: x1T_lo[:, g, k, :], w)\
                            .then_inc(made, 1)

                def scores(g, half):
                    if (g, half) == (0, 0):
                        pe.wait_ge(maska_set, pa + 1)
                        pe.wait_ge(q_set, 3 * pa + 3)
                        pe.wait_ge(k_set, 3 * pa + 3)
                    ring_wait(pe, f"s{g}{half}", t, static)
                    bank = ring_bank(f"s{g}{half}")[:, 0:G0 * P]
                    pe.matmul(bank.rearrange("p (h m) -> p h m", h=G0), idh[:],
                              mask_a[:, g:g + 1, :].to_broadcast([P, G0, P]), start=True, stop=False,
                              skip_group_check=True)
                    feats = slice(half * DH0, (half + 1) * DH0)
                    for k in range(G0):
                        mm = pe.matmul(bank[:, k * P:(k + 1) * P], qT[feats, k, g, :], kT[feats, k, g, :],
                                       start=False, stop=(k == G0 - 1), skip_group_check=True)
                    mm.then_inc(s_made, 1)

                def transpose_probs(g, half):
                    pe.wait_ge(norm_set, 4 * pa + 2 * g + half + 1)
                    ring_wait(pe, f"pT{g}{half}", t, static)
                    for k in range(G0):
                        mm = pe.transpose(ring_bank(f"pT{g}{half}")[:, k * P:(k + 1) * P], prob[:, g, half * G0 + k, :], idf[:])
                    mm.then_inc(pT_made, 1)

                def transpose_tanh(g):
                    pe.wait_ge(th_set, 2 * pb + g + 1)
                    ring_wait(pe, f"thT{g}", t, static)
                    for k in range(C):
                        mm = pe.transpose(ring_bank(f"thT{g}")[:, k * P:(k + 1) * P], th[:, g, k * P:(k + 1) * P], idf[:])
                    mm.then_inc(thT_made, 1)

                def source_and_target():
                    ring_wait(pe, "sd", t, static)
                    for g in range(PAIR):
                        pe.wait_ge(thT_set, 2 * pb + g + 1)
                        for k in range(C):
                            mm = pe.matmul(ring_bank("sd")[:, g * SD:(g + 1) * SD], thT[:, g, k, :], wsd[:, k, :],
                                           start=(k == 0), stop=(k == C - 1))
                    mm.then_inc(sd_made, 1)

                def transpose_terms():
                    pe.wait_ge(part_set, 5 * pb + 5)
                    for g in range(PAIR):
                        mm = pe.transpose(ring_bank("sd")[0:ROWS, 128 + g * 64:128 + (g + 1) * 64].bitcast(BF16),
                                          sd_parts[:, g, :, :].rearrange("p a s -> p (a s)"), idh[:])
                    mm.then_inc(sdT_made, 1)

                def logits(g, j):
                    if (g, j) == (0, 0):
                        pe.wait_ge(maskb_set, pb + 1)
                        pe.wait_ge(sdT_set, pb + 1)
                    logit_wait(pe, j, f"z{g}", t, static)
                    bank = logit[j][:].rearrange("p (h m) -> p h m", h=G1)
                    pe.matmul(bank, idh[:], mask_b[:, g:g + 1, :].to_broadcast([P, G1, P]), start=True, stop=False,
                              skip_group_check=True)
                    pe.matmul(logit[j][:], sdT[:, g, :], picks[:, G1 * j:G1 * j + G1, :].rearrange("p h m -> p (h m)"),
                              start=False, stop=False, skip_group_check=True)
                    for k in range(G1):
                        mm = pe.matmul(bank[:, k, :], pickd[:, G1 * j + k, :], sdT[:, g, :], start=False,
                                       stop=(k == G1 - 1), skip_group_check=True)
                    mm.then_inc(z_made, 1)

                def transpose_attention(g):
                    for j in range(NZ):
                        pe.wait_ge(att_set, 6 * pc + 3 * g + j + 1)
                        logit_wait(pe, j, f"aT{g}", t, static)
                        for k in range(G1):
                            mm = pe.transpose(logit[j][:, k * P:(k + 1) * P], att[:, g, G1 * j + k, :], idf[:])
                        mm.then_inc(aT_made, 1)

                def aggregate(g):
                    ring_wait(pe, f"agg{g}", t, static)
                    for h in range(HEADS1):
                        if h % G1 == 0:
                            pe.wait_ge(aT_set, 6 * pc + 3 * g + h // G1 + 1)
                        mm = pe.matmul(ring_bank(f"agg{g}")[:, h * AUG:(h + 1) * AUG], attT[:, g, h, :], h_aug[:, g, h, :],
                                       start=True, stop=True)
                    mm.then_inc(agg_made, 1)

                if a:
                    transpose_x(0)
                    transpose_x(1)
                if b:
                    context(0)
                    context(1)
                if a:
                    qk(0)
                if b:
                    out_projection(0)
                    out_projection(1)
                if a:
                    qk(1)
                if c:
                    transpose_attention(0)
                    aggregate(0)
                if a:
                    qk(2)
                if b:
                    transpose_x1(0)
                    transpose_x1(1)
                if a:
                    value(0)
                    value(1)
                if c:
                    transpose_attention(1)
                    aggregate(1)
                if b:
                    hidden_and_gate(0)
                    hidden_and_gate(1)
                if a:
                    for g in range(PAIR):
                        scores(g, 0)
                        scores(g, 1)
                if b:
                    transpose_tanh(0)
                    transpose_tanh(1)
                    source_and_target()
                if a:
                    transpose_probs(0, 0)
                    transpose_probs(0, 1)
                if b:
                    transpose_terms()
                    for j in range(NZ):
                        logits(0, j)
                if a:
                    transpose_probs(1, 0)
                    transpose_probs(1, 1)
                if b:
                    for j in range(NZ):
                        logits(1, j)

            pe.wait_ge(const_in, 16 * N_CONST)
            pe.wait_ge(w_split, 6)
            pe.wait_ge(ones_set, 1)
            run_ticks(pe, tick)

        @block.scalar
        def _(act):
            def tick(t, static, a, b, c):
                pa, pb, pc = t, t - 1, t - 2

                def round_x(g):
                    act.wait_ge(xT_made, 2 * pa + g + 1)
                    act.activation(xT_hi[:, :, g, :], ring_bank(f"xT{g}")[:, 0:D].rearrange("p (c n) -> p c n", c=C),
                                   ACT.Copy).then_inc(xhi_set, 1)

                def round_context(g):
                    act.wait_ge(ctx_made, 2 * pb + g + 1)
                    act.activation(ctxT_hi[:, g, :, :].rearrange("p c n -> p (c n)"), ring_bank(f"ctx{g}")[:, 0:D],
                                   ACT.Copy).then_inc(chi_set, 1)

                def query(k):
                    act.wait_ge(qk_made, 3 * pa + k + 1)
                    act.activation(qT[:, k, :, :].rearrange("p g n -> p (g n)"), ring_bank(f"qk{k}")[:, 0:PAIR * P],
                                   ACT.Identity, bias=cols[:, 0, k:k + 1], scale=Q_SCALE)\
                        .then_inc(q_set, 1)

                def attention_exp(g, j):
                    act.wait_ge(shift_set, 6 * pc + 3 * g + j + 1)
                    heads = att[:, g, G1 * j:G1 * j + G1, :]
                    act.activation(heads, heads, ACT.Exp).then_inc(att_set, 1)

                def round_x1(g):
                    act.wait_ge(x1T_made, 2 * pb + g + 1)
                    act.activation(x1T_hi[:, g, :, :].rearrange("p c n -> p (c n)"), ring_bank(f"x1T{g}")[:, 0:D],
                                   ACT.Copy).then_inc(x1hi_set, 1)

                def elu_exp(g):
                    act.wait_ge(fneg_set, 2 * pc + g + 1)
                    act.activation(f_exp[:, g, :], f_neg[:, g, :], ACT.Exp).then_inc(fexp_set, 1)

                def tanh_hidden(g):
                    act.wait_ge(h_made, 2 * pb + g + 1)
                    act.activation(th[:, g, :], ring_bank(f"h{g}")[:, 0:D], ACT.Tanh).then_inc(th_set, 1)

                def tanh_gate(g):
                    act.wait_ge(gpre_set, 2 * pb + g + 1)
                    act.activation(g_tanh[:, g, :], g_pre[:, g, :], ACT.Tanh, scale=0.5).then_inc(gtanh_set, 1)

                def score_exp(g, half):
                    act.wait_ge(max_set, 4 * pa + 2 * g + half + 1)
                    for k in range(G0):
                        n = half * G0 + k
                        op = act.activation(prob[:, g, n, :], ring_bank(f"s{g}{half}")[:, k * P:(k + 1) * P], ACT.Exp,
                                            bias=neg_max[:, g, n:n + 1], accum_out=p_sum[:, g, n:n + 1])
                    op.then_inc(prob_set, 1)

                def keep_tanhT(g):
                    act.wait_ge(thT_made, 2 * pb + g + 1)
                    act.activation(thT[:, g, :, :].rearrange("p c n -> p (c n)"), ring_bank(f"thT{g}")[:, 0:D],
                                   ACT.Copy).then_inc(thT_set, 1)

                def relu_logits(g, j):
                    act.wait_ge(z_made, 6 * pb + 3 * g + j + 1)
                    act.activation(z_relu[:, g, G1 * j:G1 * j + G1, :].rearrange("p h m -> p (h m)"), logit[j][:],
                                   ACT.Relu, scale=1.0 - SLOPE).then_inc(relu_set, 1)

                if a:
                    round_x(0)
                    round_x(1)
                if b:
                    round_context(0)
                    round_context(1)
                if c:
                    for j in range(NZ):
                        attention_exp(0, j)
                if a:
                    query(0)
                    query(1)
                if c:
                    for j in range(NZ):
                        attention_exp(1, j)
                if a:
                    query(2)
                if b:
                    round_x1(0)
                    round_x1(1)
                if c:
                    elu_exp(0)
                    elu_exp(1)
                if b:
                    for g in range(PAIR):
                        tanh_hidden(g)
                        tanh_gate(g)
                if a:
                    score_exp(0, 0)
                    score_exp(0, 1)
                if b:
                    keep_tanhT(0)
                    keep_tanhT(1)
                if a:
                    score_exp(1, 0)
                    score_exp(1, 1)
                if b:
                    for g in range(PAIR):
                        for j in range(NZ):
                            relu_logits(g, j)

            act.wait_ge(bq_scaled, 1)
            run_ticks(act, tick)

        @block.vector
        def _(dve):
            for n in range(6):
                dve.wait_ge(w_in, 16 * n + 16)
                dve.tensor_copy(w_hi[:, n, :, :], w_f32[:]).then_inc(w_rounded, 1)
                dve.wait_ge(w_rounded, n + 1)
                dve.tensor_tensor(w_lo[:, n, :, :], w_f32[:], w_hi[:, n, :, :].bitcast(F32), ALU.subtract)\
                    .then_inc(w_split, 1)
            dve.wait_ge(const_in, 16 * N_CONST)
            dve.tensor_scalar(cols[:, 0, :], cols[:, 0, :], Q_SCALE, None, ALU.mult).then_inc(bq_scaled, 1)

            def tick(t, static, a, b, c):
                pa, pb, pc = t, t - 1, t - 2

                def keep_mask():
                    if static is None or pb > 0:
                        dve.wait_ge(z_made, 6 * pb)
                    dve.wait_ge(maska_set, pb + 1)
                    dve.tensor_copy(mask_b[:], mask_a[:]).then_inc(maskb_set, 1)

                def make_mask():
                    dve.wait_ge(adj_loaded, 16 * pa + 16)
                    if static is None or pa > 0:
                        dve.wait_ge(s_made, 4 * pa)
                        dve.wait_ge(maskb_set, pa)
                    dve.tensor_scalar(mask_a[:], adj_in[:], -1.0, -MASKED, ALU.add, ALU.mult).then_inc(maska_set, 1)

                def rest_x(g):
                    dve.wait_ge(xhi_set, 2 * pa + g + 1)
                    dve.tensor_tensor(xT_lo[:, :, g, :], ring_bank(f"xT{g}")[:, 0:D].rearrange("p (c n) -> p c n", c=C),
                                      xT_hi[:, :, g, :].bitcast(F32), ALU.subtract).then_inc(xlo_set, 1)

                def rest_context(g):
                    dve.wait_ge(chi_set, 2 * pb + g + 1)
                    dve.tensor_tensor(ctxT_lo[:, g, :, :].rearrange("p c n -> p (c n)"), ring_bank(f"ctx{g}")[:, 0:D],
                                      ctxT_hi[:, g, :, :].rearrange("p c n -> p (c n)").bitcast(F32), ALU.subtract)\
                       .then_inc(clo_set, 1)

                def key(k):
                    dve.wait_ge(q_set, C * pa + k + 1)
                    dve.tensor_scalar(kT[:, k, :, :].rearrange("p g n -> p (g n)"), ring_bank(f"qk{k}")[:, PAIR * P:2 * PAIR * P],
                                      cols[:, 1, k:k + 1], None, ALU.add).then_inc(k_set, 1)

                def residual(g):
                    dve.wait_ge(out_made, 2 * pb + g + 1)
                    dve.wait_ge(xres_set, 2 * pb + g + 1)
                    dve.tensor_tensor(y0[:, g, :], ring_bank(f"out{g}")[:, 0:D], x_res[:, g, :], ALU.add).then_inc(y0_set, 1)
                    dve.wait_ge(y0_set, 2 * pb + g + 1)
                    dve.bn_stats(stats0[:, g, :], y0[:, g, :]).then_inc(st0_set, 1)

                def aggregate0(g):
                    dve.bn_aggr(mv0[:, g, :], stats0[:, g, :]).then_inc(mv0_set, 1)

                def normalize0(g):
                    dve.wait_ge(rstd0_set, 2 * pb + g + 1)
                    dve.tensor_scalar(x1[:, g, :], y0[:, g, :], mv0[:, g, 0:1], rstd0[:, g:g + 1], ALU.subtract, ALU.mult)\
                       .then_inc(x1_set, 1)

                def rest_x1(g):
                    dve.wait_ge(x1hi_set, 2 * pb + g + 1)
                    dve.tensor_tensor(x1T_lo[:, g, :, :].rearrange("p c n -> p (c n)"), ring_bank(f"x1T{g}")[:, 0:D],
                                      x1T_hi[:, g, :, :].rearrange("p c n -> p (c n)").bitcast(F32), ALU.subtract)\
                       .then_inc(x1lo_set, 1)

                def value(g):
                    dve.wait_ge(v_made, 2 * pa + g + 1)
                    dve.tensor_tensor(v[:, g, :], ring_bank(f"v{g}")[:, 0:D], rows[:, BV, :], ALU.add).then_inc(v_set, 1)

                def hidden(g):
                    dve.wait_ge(th_set, 2 * pb + g + 1)
                    dve.tensor_tensor(h_aug[:, g, :, 0:DH1], ring_bank(f"h{g}")[:, 0:D].rearrange("p (h e) -> p h e", h=HEADS1),
                                      rows[:, BH, :].rearrange("p (h e) -> p h e", h=HEADS1), ALU.add).then_inc(h_set, 1)

                def gate_bias(g):
                    dve.wait_ge(g_made, 2 * pb + g + 1)
                    dve.tensor_tensor(g_pre[:, g, :], ring_bank(f"g{g}")[:, 0:D], rows[:, BG, :], ALU.add).then_inc(gpre_set, 1)

                def score_max(g, half):
                    dve.wait_ge(s_made, 4 * pa + 2 * g + half + 1)
                    dve.tensor_reduce(neg_max[:, g, half * G0:(half + 1) * G0],
                                      ring_bank(f"s{g}{half}")[:, 0:G0 * P].rearrange("p (h m) -> p h m", h=G0),
                                      AX.X, ALU.max, negate=True).then_inc(max_set, 1)

                def invert_sum(g, half):
                    dve.wait_ge(prob_set, 4 * pa + 2 * g + half + 1)
                    heads = slice(half * G0, (half + 1) * G0)
                    dve.reciprocal(p_inv[:, g, heads], p_sum[:, g, heads]).then_inc(inv_set, 1)

                def keep_probT(g, half):
                    dve.wait_ge(pT_made, 4 * pa + 2 * g + half + 1)
                    dve.tensor_copy(probT[:, g, half * G0:(half + 1) * G0, :].rearrange("p h n -> p (h n)"),
                                    ring_bank(f"pT{g}{half}")[:, 0:G0 * P]).then_inc(pT_set, 1)

                def split_terms():
                    dve.wait_ge(sd_made, pb + 1)
                    terms = ring_bank("sd")[:, 0:PAIR * SD].rearrange("p (g s) -> p g s", g=PAIR)
                    dve.tensor_copy(sd_parts[:, :, 0, :], terms).then_inc(part_set, 1)
                    dve.wait_ge(part_set, 5 * pb + 1)
                    dve.tensor_tensor(sd_rest[:], terms, sd_parts[:, :, 0, :], ALU.subtract).then_inc(part_set, 1)
                    dve.wait_ge(part_set, 5 * pb + 2)
                    dve.tensor_copy(sd_parts[:, :, 1, :], sd_rest[:]).then_inc(part_set, 1)
                    dve.wait_ge(part_set, 5 * pb + 3)
                    dve.tensor_tensor(sd_rest2[:], sd_rest[:], sd_parts[:, :, 1, :], ALU.subtract).then_inc(part_set, 1)
                    dve.wait_ge(part_set, 5 * pb + 4)
                    dve.tensor_copy(sd_parts[:, :, 2, :], sd_rest2[:]).then_inc(part_set, 1)

                def keep_terms():
                    dve.wait_ge(sdT_made, pb + 1)
                    dve.tensor_copy(sdT[:].rearrange("p g n -> p (g n)"),
                                    ring_bank("sd")[0:ROWS, 128:128 + PAIR * P // 2].bitcast(BF16)).then_inc(sdT_set, 1)

                def leaky(g, j):
                    n = 6 * pb + 3 * g + j + 1
                    heads = slice(G1 * j, G1 * j + G1)
                    dve.wait_ge(relu_set, n)
                    dve.scalar_tensor_tensor(out=att[:, g, heads, :].rearrange("p h m -> p (h m)"), in0=logit[j][:], scalar=SLOPE,
                                             in1=z_relu[:, g, heads, :].rearrange("p h m -> p (h m)"),
                                             op0=ALU.mult, op1=ALU.add).then_inc(leaky_set, 1)
                    dve.wait_ge(leaky_set, n)
                    dve.tensor_reduce(att_max[:, g, heads], att[:, g, heads, :], AX.X, ALU.max).then_inc(amax_set, 1)

                def keep_attT(g):
                    for j in range(NZ):
                        dve.wait_ge(aT_made, 6 * pc + 3 * g + j + 1)
                        dve.tensor_copy(attT[:, g, G1 * j:G1 * j + G1, :].rearrange("p h n -> p (h n)"), logit[j][:])\
                           .then_inc(aT_set, 1)

                def weigh(g):
                    dve.wait_ge(agg_made, 2 * pc + g + 1)
                    sums = ring_bank(f"agg{g}")[:, 0:HEADS1 * AUG].rearrange("p (h e) -> p h e", h=HEADS1)
                    dve.reciprocal(a_inv[:, g, :], sums[:, :, DH1]).then_inc(ainv_set, 1)
                    dve.wait_ge(ainv_set, 2 * pc + g + 1)
                    dve.tensor_tensor(f[:, g, :].rearrange("p (h e) -> p h e", h=HEADS1), sums[:, :, 0:DH1],
                                      a_inv[:, g, :].unsqueeze(2).to_broadcast([P, HEADS1, DH1]), ALU.mult).then_inc(f_set, 1)
                    dve.wait_ge(f_set, 2 * pc + g + 1)
                    dve.tensor_scalar(f_neg[:, g, :], f[:, g, :], 0.0, None, ALU.min).then_inc(fneg_set, 1)

                def elu_and_gate(g):
                    dve.wait_ge(fexp_set, 2 * pc + g + 1)
                    dve.scalar_tensor_tensor(out=elu1[:, g, :], in0=f[:, g, :], scalar=0.0, in1=f_exp[:, g, :],
                                             op0=ALU.max, op1=ALU.add).then_inc(elu_set, 1)
                    dve.wait_ge(elu_set, 2 * pc + g + 1)
                    dve.wait_ge(gate_set, 2 * pc + g + 1)
                    dve.scalar_tensor_tensor(out=gated[:, g, :], in0=elu1[:, g, :], scalar=-1.0, in1=gate[:, g, :],
                                             op0=ALU.add, op1=ALU.mult).then_inc(gated_set, 1)

                def gate_value(g):
                    dve.wait_ge(gtanh_set, 2 * pb + g + 1)
                    dve.tensor_scalar(gate[:, g, :], g_tanh[:, g, :], 0.5, 0.5, ALU.mult, ALU.add).then_inc(gate_set, 1)

                def ungated(g):
                    dve.wait_ge(gate_set, 2 * pb + g + 1)
                    dve.scalar_tensor_tensor(out=gx[:, g, :], in0=gate[:, g, :], scalar=-2.0, in1=x1[:, g, :],
                                             op0=ALU.add, op1=ALU.mult).then_inc(gx_set, 1)

                def moments1(g):
                    dve.wait_ge(y1_set, 2 * pc + g + 1)
                    dve.bn_stats(stats1[:, g, :], y1[:, g, :]).then_inc(st1_set, 1)

                def aggregate1(g):
                    dve.bn_aggr(mv1[:, g, :], stats1[:, g, :]).then_inc(mv1_set, 1)

                def normalize1(g):
                    if g == 0 and (static is None or pc > 0):
                        dve.wait_ge(stored, 16 * pc)
                    dve.wait_ge(rstd1_set, 2 * pc + g + 1)
                    dve.tensor_scalar(y_out[:, g, :], y1[:, g, :], mv1[:, g, 0:1], rstd1[:, g:g + 1], ALU.subtract, ALU.mult)\
                       .then_inc(yout_set, 1)

                if b:
                    keep_mask()
                if a:
                    make_mask()
                    rest_x(0)
                    rest_x(1)
                if b:
                    rest_context(0)
                    rest_context(1)
                if a:
                    key(0)
                if b:
                    residual(0)
                    residual(1)
                    dve.wait_ge(st0_set, 2 * pb + 2)
                if a:
                    key(1)
                if b:
                    aggregate0(0)
                    aggregate0(1)
                if c:
                    keep_attT(0)
                if b:
                    normalize0(0)
                    normalize0(1)
                if c:
                    weigh(0)
                if a:
                    key(2)
                if b:
                    rest_x1(0)
                    rest_x1(1)
                if c:
                    elu_and_gate(0)
                if a:
                    value(0)
                    value(1)
                if c:
                    moments1(0)
                    dve.wait_ge(st1_set, 2 * pc + 1)
                    keep_attT(1)
                    aggregate1(0)
                    weigh(1)
                    normalize1(0)
                    elu_and_gate(1)
                if b:
                    hidden(0)
                    gate_bias(0)
                if c:
                    moments1(1)
                    dve.wait_ge(st1_set, 2 * pc + 2)
                if b:
                    hidden(1)
                    gate_bias(1)
                if c:
                    aggregate1(1)
                if b:
                    gate_value(0)
                if c:
                    normalize1(1)
                if a:
                    for g in range(PAIR):
                        score_max(g, 0)
                        score_max(g, 1)
                    invert_sum(0, 0)
                    invert_sum(0, 1)
                if b:
                    gate_value(1)
                    ungated(0)
                    ungated(1)
                    split_terms()
                if a:
                    keep_probT(0, 0)
                    keep_probT(0, 1)
                    invert_sum(1, 0)
                    invert_sum(1, 1)
                if b:
                    keep_terms()
                    for j in range(NZ):
                        leaky(0, j)
                if a:
                    keep_probT(1, 0)
                    keep_probT(1, 1)
                if b:
                    for j in range(NZ):
                        leaky(1, j)

            dve.memset(h_aug[:, :, :, DH1:AUG], 1.0).then_inc(ones_set, 1)
            run_ticks(dve, tick)

        @block.gpsimd
        def _(pool):
            def tick(t, static, a, b, c):
                pa, pb, pc = t, t - 1, t - 2

                def residual_input(g):
                    if g == 0:
                        pool.wait_ge(x_loaded, 16 * pa + 16)
                    if static is None or pa > 0:
                        pool.wait_ge(y0_set, 2 * (pa - 1) + g + 1)
                    pool.tensor_tensor(x_res[:, g, :], x_in[:, g, :], rows[:, BF, :], ALU.add).then_inc(xres_set, 1)

                def inverse_deviation(g, mv, ve, rstd, mv_set, ve_set, rstd_set, pair):
                    pool.wait_ge(mv_set, 2 * pair + g + 1)
                    pool.tensor_tensor(ve[:, g:g + 1], mv[:, g, 1:2], eps[:], ALU.add).then_inc(ve_set, 1)
                    pool.wait_ge(ve_set, 2 * pair + g + 1)
                    pool.tensor_tensor(rstd[:, g:g + 1], ve[:, g:g + 1], neg_half[:], ALU.pow).then_inc(rstd_set, 1)

                def gated_sum(g):
                    pool.wait_ge(gated_set, 2 * pc + g + 1)
                    pool.wait_ge(gx_set, 2 * pc + g + 1)
                    pool.tensor_tensor(y1[:, g, :], gated[:, g, :], gx[:, g, :], ALU.subtract).then_inc(y1_set, 1)

                def normalize_probs(g, half):
                    pool.wait_ge(inv_set, 4 * pa + 2 * g + half + 1)
                    heads = slice(half * G0, (half + 1) * G0)
                    pool.tensor_tensor(prob[:, g, heads, :], prob[:, g, heads, :],
                                       p_inv[:, g, heads].unsqueeze(2).to_broadcast([P, G0, P]), ALU.mult).then_inc(norm_set, 1)

                def shift_attention(g, j):
                    pool.wait_ge(amax_set, 6 * pb + 3 * g + j + 1)
                    heads = slice(G1 * j, G1 * j + G1)
                    pool.tensor_tensor(att[:, g, heads, :], att[:, g, heads, :],
                                       att_max[:, g, heads].unsqueeze(2).to_broadcast([P, G1, P]), ALU.subtract)\
                        .then_inc(shift_set, 1)

                if b:
                    inverse_deviation(0, mv0, ve0, rstd0, mv0_set, ve0_set, rstd0_set, pb)
                    inverse_deviation(1, mv0, ve0, rstd0, mv0_set, ve0_set, rstd0_set, pb)
                if a:
                    residual_input(0)
                    residual_input(1)
                if c:
                    for g in range(PAIR):
                        gated_sum(g)
                        inverse_deviation(g, mv1, ve1, rstd1, mv1_set, ve1_set, rstd1_set, pc)
                if a:
                    for g in range(PAIR):
                        normalize_probs(g, 0)
                        normalize_probs(g, 1)
                if b:
                    for g in range(PAIR):
                        for j in range(NZ):
                            shift_attention(g, j)

            pool.wait_ge(const_in, 16 * N_CONST)
            pool.memset(neg_half[:], -0.5).then_inc(half_set, 1)
            pool.memset(eps[:], EPS).then_inc(half_set, 1)
            pool.wait_ge(half_set, 2)
            run_ticks(pool, tick)


def kernel(**inputs):
    import concourse.bacc as bacc
    import ml_dtypes
    import numpy as np
    from concourse.bass_utils import run_bass_kernel_spmd

    def arr(name):
        return np.asarray(inputs[name])

    def by_partition(w):
        return w.reshape(-1, P, w.shape[-1]).transpose(1, 0, 2)

    x, adj = arr("x"), arr("adj")
    D = x.shape[-1]
    W, w_src, w_dst = arr("L1_gnn_W"), arr("L1_gnn_w_src"), arr("L1_gnn_w_dst")
    heads, _, dh = W.shape
    w_sd = np.zeros((D, 2 * heads), W.dtype)
    for h in range(heads):
        w_sd[h * dh:(h + 1) * dh, h] = w_src[h, :, 0]
        w_sd[h * dh:(h + 1) * dh, heads + h] = w_dst[h, :, 0]
    row = np.arange(PARTS * 2 * heads) % (2 * heads)
    pick = (row[:, None] == np.arange(2 * heads)[None, :])[:, :, None] & np.ones(P, bool)
    arrays = {
        "x": x,
        "adj": adj.transpose(1, 0, 2),
        "weights": np.stack([by_partition(w) for w in (
            arr("L0_gnn_Wq"), arr("L0_gnn_Wk"), arr("L0_gnn_Wv"), arr("L0_gnn_Wf"),
            W.transpose(1, 0, 2).reshape(D, -1), arr("L1_gnn_H_w").T)]),
        "bias_rows": np.stack([np.broadcast_to(b, (P, D)) for b in (
            arr("L0_gnn_bv"), arr("L0_gnn_bf"), np.tile(arr("L1_gnn_b"), heads), arr("L1_gnn_H_b"))], axis=1),
        "bias_cols": np.stack([arr(n).reshape(-1, P).T for n in ("L0_gnn_bq", "L0_gnn_bk")], axis=1),
        "w_sd": by_partition(w_sd),
        "ident": np.eye(P, dtype=np.float32),
        "ident_h": np.eye(P, dtype=ml_dtypes.bfloat16),
        "pick_s": pick[:, :heads].astype(ml_dtypes.bfloat16),
        "pick_d": pick[:, heads:].astype(ml_dtypes.bfloat16),
    }
    arrays = {n: np.ascontiguousarray(a) for n, a in arrays.items()}
    nc = bacc.Bacc("TRN2", target_bir_lowering=False, num_devices=1)
    args = [nc.dram_tensor(n, a.shape, mybir.dt.from_np(a.dtype), kind="ExternalInput").ap() for n, a in arrays.items()]
    out = nc.dram_tensor("out", x.shape, F32, kind="ExternalOutput").ap()
    build(nc, *args, out)
    result = run_bass_kernel_spmd(nc, [arrays], core_ids=[0])
    return result.results[0]["out"]
```

```python
from contextlib import ExitStack

import concourse.bass as bass
from concourse import mybir

F32 = mybir.dt.float32
F32R = mybir.dt.float32r
BF16 = mybir.dt.bfloat16
U8 = mybir.dt.uint8
ALU = mybir.AluOpType
ACT = mybir.ActivationFunctionType
AX = mybir.AxisListType

P = 128
PAIR = 2
HEADS0 = 6
HEADS1 = 12
PARTS = 3
MASKED = -9.0e15
EPS = 1e-5
SLOPE = 0.2

RING = 4
JOBS = [
    ("qk0", "A"), ("ctx0", "B"), ("ctx1", "B"), ("qk1", "A"), ("out0", "B"), ("out1", "B"),
    ("qk2", "A"), ("x1T0", "B"), ("x1T1", "B"), ("agg0", "C"), ("s00", "A"), ("s01", "A"),
    ("h0", "B"), ("f0", "C"), ("g0", "B"), ("agg1", "C"), ("h1", "B"), ("s10", "A"),
    ("s11", "A"), ("f1", "C"), ("v0", "A"), ("pT00", "A"), ("pT01", "A"), ("v1", "A"),
    ("sdT", "B"), ("g1", "B"), ("pT10", "A"), ("pT11", "A"),
]
SLOT = {name: k for k, (name, _) in enumerate(JOBS)}
RING1 = 4
JOBS1 = [(f"{kind}{g}{j}", stage) for kind, stage in (("aT", "C"), ("z", "B")) for g in range(2) for j in range(3)]
SLOT1 = {name: k for k, (name, _) in enumerate(JOBS1)}
LAG = {"A": 0, "B": 1, "C": 2}


def tenant_before(jobs, name, tick, pairs):
    at = [n for n, _ in jobs].index(name)
    if pairs is None:
        n, stage = jobs[at - 1]
        return n, tick - LAG[stage] - (at == 0)
    earlier = [(tick, job) for job in jobs[:at]]
    for back in range(1, 4):
        earlier = [(tick - back, job) for job in jobs] + earlier
    for at_tick, (n, stage) in reversed(earlier):
        if 0 <= at_tick - LAG[stage] < pairs:
            return n, at_tick - LAG[stage]
    return None


def build(nc, x, xT, adj, weights, bias_rows, bias_cols, ident, ident_h, pick_s, pick_d, out):
    B, _, D = x.shape
    C = D // P
    DH0 = D // HEADS0
    DH1 = D // HEADS1
    NP = B // PAIR
    G0 = HEADS0 // 2
    G1 = 4
    NZ = HEADS1 // G1
    SD = 2 * HEADS1
    ROWS = PARTS * SD
    Q_SCALE = float(DH0) ** -0.5
    WQ, WK, WV, WF, WH, WG = range(6)
    BF, BH, BG, W_SRC, W_DST = range(5)
    assert NP > 5 and C * P == D and NZ == 3

    with ExitStack() as ctx:
        def sb(name, shape, dt=F32):
            return ctx.enter_context(nc.sbuf_tensor(name, shape, dt))

        def sem(name):
            return ctx.enter_context(nc.semaphore(name))

        ring = [ctx.enter_context(nc.psum_tensor(f"ring{k}", [P, 512], F32)) for k in range(RING)]
        logit = [ctx.enter_context(nc.psum_tensor(f"logit{k}", [P, 512], F32)) for k in range(RING1)]

        w_f32 = sb("w_f32", [P, C, D])
        w_hi = sb("w_hi", [P, 6, C, D], F32R)
        w_lo = sb("w_lo", [P, 6, C, D], F32R)
        rows = sb("rows", [P, 5, D])
        cols = sb("cols", [P, 3, C])
        idf = sb("idf", [P, P])
        idh = sb("idh", [P, P], BF16)
        picks = sb("picks", [ROWS, HEADS1, P], BF16)
        pickd = sb("pickd", [ROWS, HEADS1, P], BF16)
        neg_half = sb("neg_half", [P, 1])
        eps = sb("eps", [P, 1])
        xT_in = sb("xT_in", [P, C, PAIR, P])
        x_in = sb("x_in", [P, PAIR, D])
        adj_in = sb("adj_in", [P, PAIR, P], U8)
        mask_a = sb("mask_a", [P, PAIR, P], BF16)
        x_res = sb("x_res", [P, PAIR, D])
        xT_hi = sb("xT_hi", [P, C, PAIR, P], F32R)
        xT_lo = sb("xT_lo", [P, C, PAIR, P], F32R)
        qT = sb("qT", [P, C, PAIR, P])
        kT = sb("kT", [P, C, PAIR, P])
        v = sb("v", [P, PAIR, D])
        neg_max = sb("neg_max", [P, PAIR, HEADS0])
        p_sum = sb("p_sum", [P, PAIR, HEADS0])
        p_inv = sb("p_inv", [P, PAIR, HEADS0])
        prob = sb("prob", [P, PAIR, HEADS0, P])
        probT = sb("probT", [P, PAIR, HEADS0, P])
        mask_b = sb("mask_b", [P, PAIR, P], BF16)
        ctxT_hi = sb("ctxT_hi", [P, PAIR, C, P], F32R)
        ctxT_lo = sb("ctxT_lo", [P, PAIR, C, P], F32R)
        x1 = sb("x1", [P, PAIR, D])
        stats0 = sb("stats0", [P, PAIR, 6])
        mv0 = sb("mv0", [P, PAIR, 2])
        ve0 = sb("ve0", [P, PAIR])
        rstd0 = sb("rstd0", [P, PAIR])
        x1T_hi = sb("x1T_hi", [P, PAIR, C, P], F32R)
        x1T_lo = sb("x1T_lo", [P, PAIR, C, P], F32R)
        h = sb("h", [P, PAIR, D])
        th = sb("th", [P, PAIR, D])
        th_w = sb("th_w", [P, PAIR, 2, D])
        terms = sb("terms", [P, PAIR, SD])
        g_tanh = sb("g_tanh", [P, PAIR, D])
        gate = sb("gate", [P, PAIR, D])
        gx = sb("gx", [P, PAIR, D])
        sd_parts = sb("sd_parts", [P, PAIR, PARTS, SD], BF16)
        sd_rest = sb("sd_rest", [P, PAIR, SD])
        sd_rest2 = sb("sd_rest2", [P, PAIR, SD])
        sdT = sb("sdT", [ROWS, PAIR, P], BF16)
        att = sb("att", [P, PAIR, HEADS1, P])
        att_min = sb("att_min", [P, PAIR, HEADS1])
        att_sum = sb("att_sum", [P, PAIR, HEADS1])
        attT = sb("attT", [P, PAIR, HEADS1, P])
        a_inv = sb("a_inv", [P, PAIR, HEADS1])
        aggT = sb("aggT", [P, PAIR, C, P])
        f = sb("f", [P, PAIR, D])
        gated = sb("gated", [P, PAIR, D])
        y1 = sb("y1", [P, PAIR, D])
        stats1 = sb("stats1", [P, PAIR, 6])
        mv1 = sb("mv1", [P, PAIR, 2])
        ve1 = sb("ve1", [P, PAIR])
        rstd1 = sb("rstd1", [P, PAIR])
        y_out = sb("y_out", [P, PAIR, D])

        const_in = sem("const_in")
        w_in = sem("w_in")
        w_rounded = sem("w_rounded")
        w_split = sem("w_split")
        bq_scaled = sem("bq_scaled")
        half_set = sem("half_set")
        bv_made, bf_set = sem("bv_made"), sem("bf_set")
        x_loaded = sem("x_loaded")
        xT_loaded = sem("xT_loaded")
        adj_loaded = sem("adj_loaded")
        stored = sem("stored")
        qk_made, v_made = sem("qk_made"), sem("v_made")
        s_made, pT_made, ctx_made = sem("s_made"), sem("pT_made"), sem("ctx_made")
        out_made, x1T_made, h_made = sem("out_made"), sem("x1T_made"), sem("h_made")
        g_made, sdT_made, z_made = sem("g_made"), sem("sdT_made"), sem("z_made")
        aT_made, agg_made, f_made = sem("aT_made"), sem("agg_made"), sem("f_made")
        xhi_set, xlo_set, q_set, k_set, v_set = (sem(n) for n in ("xhi_set", "xlo_set", "q_set", "k_set", "v_set"))
        max_set, prob_set, inv_set, norm_set, pT_set = (sem(n) for n in ("max_set", "prob_set", "inv_set", "norm_set", "pT_set"))
        chi_set, clo_set, y0_set, st0_set, mv0_set = (sem(n) for n in ("chi_set", "clo_set", "y0_set", "st0_set", "mv0_set"))
        ve0_set, rstd0_set, x1_set, x1hi_set, x1lo_set = (sem(n) for n in ("ve0_set", "rstd0_set", "x1_set", "x1hi_set", "x1lo_set"))
        h_set, th_set, thw_set, gpre_set, gtanh_set = (sem(n) for n in ("h_set", "th_set", "thw_set", "gpre_set", "gtanh_set"))
        gate_set, gx_set, terms_set, part_set, rest_set, sdT_set = (
            sem(n) for n in ("gate_set", "gx_set", "terms_set", "part_set", "rest_set", "sdT_set"))
        relu_set = [sem(f"relu{g}_set") for g in range(PAIR)]
        leaky_set, att_set = sem("leaky_set"), sem("att_set")
        aT_set, ainv_set, aggT_set, f_set, fneg_set, fexp_set = (sem(n) for n in ("aT_set", "ainv_set", "aggT_set", "f_set", "fneg_set", "fexp_set"))
        elu_set, gated_set, y1_set, st1_set, mv1_set = (sem(n) for n in ("elu_set", "gated_set", "y1_set", "st1_set", "mv1_set"))
        ve1_set, rstd1_set, yout_set = (sem(n) for n in ("ve1_set", "rstd1_set", "yout_set"))
        maska_set, maskb_set, xres_set = (sem(n) for n in ("maska_set", "maskb_set", "xres_set"))

        N_CONST = 6

        def need(eng, s, value):
            if not isinstance(value, int) or value > 0:
                eng.wait_ge(s, value)

        def run_ticks(eng, tick):
            def peeled(t):
                tick(t, NP, t < NP, 1 <= t < NP + 1, 2 <= t < NP + 2, 3 <= t)
            for t in range(4):
                peeled(t)
            with eng.Fori(4, NP - 1) as t:
                tick(t, None, True, True, True, True)
            for t in range(NP - 1, NP + 3):
                peeled(t)

        def ring_bank(name):
            return ring[SLOT[name] % RING]

        readers = {"sdT": [(sdT_set, 1, 1)]}
        for g in range(PAIR):
            readers[f"ctx{g}"] = [(clo_set, 2, g + 1)]
            readers[f"out{g}"] = [(y0_set, 2, g + 1)]
            readers[f"agg{g}"] = [(aggT_set, 2, g + 1)]
            readers[f"f{g}"] = [(f_set, 2, g + 1)]
            readers[f"x1T{g}"] = [(x1lo_set, 2, g + 1)]
            readers[f"v{g}"] = [(v_set, 2, g + 1)]
            readers[f"h{g}"] = [(h_set, 2, g + 1)]
            readers[f"g{g}"] = [(gpre_set, 2, g + 1)]
            for half in range(2):
                readers[f"s{g}{half}"] = [(prob_set, 4, 2 * g + half + 1)]
                readers[f"pT{g}{half}"] = [(pT_set, 4, 2 * g + half + 1)]
            for j in range(NZ):
                readers[f"aT{g}{j}"] = [(aT_set, 6, NZ * g + j + 1)]
                readers[f"z{g}{j}"] = [(leaky_set, 6, NZ * g + j + 1)]
        for k in range(C):
            readers[f"qk{k}"] = [(k_set, C, k + 1)]

        def wait_read(eng, tenant):
            if tenant is not None:
                name, pair = tenant
                for s, per_pair, count in readers[name]:
                    eng.wait_ge(s, per_pair * pair + count)

        def ring_wait(eng, name, t, static):
            wait_read(eng, tenant_before(JOBS[SLOT[name] % RING::RING], name, t, static))

        def logit_bank(kind, g, j):
            return logit[SLOT1[f"{kind}{g}{j}"] % RING1]

        def logit_wait(eng, kind, g, j, t, static):
            name = f"{kind}{g}{j}"
            wait_read(eng, tenant_before(JOBS1[SLOT1[name] % RING1::RING1], name, t, static))

        block = ctx.enter_context(nc.Block())

        @block.sync
        def _(sp):
            sp.dma_start(xT_in[:], xT[0]).then_inc(xT_loaded, 16)
            for n in range(6):
                need(sp, w_split, n)
                sp.dma_start(w_f32[:], weights[n]).then_inc(w_in, 16)
                if n == 0:
                    for dst, src in ((cols[:], bias_cols), (rows[:], bias_rows), (idf[:], ident), (idh[:], ident_h),
                                     (picks[:], pick_s), (pickd[:], pick_d)):
                        sp.dma_start(dst, src).then_inc(const_in, 16)
                    sp.dma_start(adj_in[:], adj[:, 0:PAIR, :]).then_inc(adj_loaded, 16)
                    sp.dma_start(x_in[:], x[0:PAIR].rearrange("b n d -> n b d")).then_inc(x_loaded, 16)
                    sp.wait_ge(xlo_set, 2)
                    sp.dma_start(xT_in[:], xT[1]).then_inc(xT_loaded, 16)

            def tick(t, static, d):
                more, after, done = (t + 1) * PAIR, t + 2, (t - 3) * PAIR
                if static is None or t + 1 < NP:
                    sp.wait_ge(maska_set, t + 1)
                    sp.wait_ge(xres_set, 2 * t + 2)
                    sp.dma_start(x_in[:], x[bass.ds(more, PAIR)].rearrange("b n d -> n b d")).then_inc(x_loaded, 16)
                    sp.dma_start(adj_in[:], adj[:, bass.ds(more, PAIR), :]).then_inc(adj_loaded, 16)
                if static is None or t + 2 < NP:
                    sp.wait_ge(xlo_set, 2 * t + 4)
                    sp.dma_start(xT_in[:], xT[after]).then_inc(xT_loaded, 16)
                if d:
                    sp.wait_ge(yout_set, 2 * (t - 3) + 2)
                    sp.dma_start(out[bass.ds(done, PAIR)].rearrange("b n d -> n b d"), y_out[:]).then_inc(stored, 16)

            for t in range(3):
                tick(t, NP, False)
            with sp.Fori(3, NP - 2) as t:
                tick(t, None, True)
            for t in range(NP - 2, NP + 3):
                tick(t, NP, True)
            sp.wait_ge(stored, 16 * NP)

        @block.tensor
        def _(pe):
            def split_product(dst, terms):
                for n, (stationary, moving) in enumerate(terms):
                    mm = pe.matmul(dst, stationary, moving, start=(n == 0), stop=(n == len(terms) - 1))
                return mm

            def rows_by_weight(name, hiT, loT, w):
                terms = []
                for k in range(C):
                    terms += [(hiT(k), w_hi[:, w, k, :]), (hiT(k), w_lo[:, w, k, :]), (loT(k), w_hi[:, w, k, :])]
                return split_product(ring_bank(name)[:, 0:D], terms)

            def tick(t, static, a, b, c, d):
                pa, pb, pc, pd = t, t - 1, t - 2, t - 3

                def context(g):
                    pe.wait_ge(pT_set, 4 * pb + 2 * g + 2)
                    ring_wait(pe, f"ctx{g}", t, static)
                    bank = ring_bank(f"ctx{g}")
                    for k in range(C):
                        for half in range(2):
                            mm = pe.matmul(bank[DH0 * half:DH0 * half + DH0, k * P:(k + 1) * P],
                                           v[:, g, (2 * k + half) * DH0:(2 * k + half + 1) * DH0],
                                           probT[:, g, half * G0 + k, :], start=True, stop=True)
                    mm.then_inc(ctx_made, 1)

                def qk(k):
                    if k == 0:
                        pe.wait_ge(xlo_set, 2 * pa + 2)
                        if static == NP and pa == 0:
                            pe.wait_ge(w_split, 2)
                    ring_wait(pe, f"qk{k}", t, static)
                    bank = ring_bank(f"qk{k}")
                    for n, w in enumerate((WQ, WK)):
                        terms = []
                        for j in range(C):
                            tile = slice(k * P, (k + 1) * P)
                            hi, lo = (xT[:, j, :, :].rearrange("p g n -> p (g n)") for xT in (xT_hi, xT_lo))
                            terms += [(w_hi[:, w, j, tile], hi), (w_hi[:, w, j, tile], lo), (w_lo[:, w, j, tile], hi)]
                        mm = split_product(bank[:, n * PAIR * P:(n + 1) * PAIR * P], terms)
                    mm.then_inc(qk_made, 1)

                def out_projection(g):
                    pe.wait_ge(clo_set, 2 * pb + g + 1)
                    if static == NP and pb == 0:
                        pe.wait_ge(w_split, 6)
                    ring_wait(pe, f"out{g}", t, static)
                    rows_by_weight(f"out{g}", lambda k: ctxT_hi[:, g, k, :], lambda k: ctxT_lo[:, g, k, :], WF)\
                        .then_inc(out_made, 1)

                def transpose_x1(g):
                    pe.wait_ge(x1_set, 2 * pb + g + 1)
                    ring_wait(pe, f"x1T{g}", t, static)
                    for k in range(C):
                        mm = pe.transpose(ring_bank(f"x1T{g}")[:, k * P:(k + 1) * P], x1[:, g, k * P:(k + 1) * P], idf[:])
                    mm.then_inc(x1T_made, 1)

                def value(g):
                    if static == NP and pa == 0:
                        pe.wait_ge(w_split, 3)
                    ring_wait(pe, f"v{g}", t, static)
                    rows_by_weight(f"v{g}", lambda k: xT_hi[:, k, g, :], lambda k: xT_lo[:, k, g, :], WV)\
                        .then_inc(v_made, 1)

                def project_value_bias():
                    pe.wait_ge(w_split, 4)
                    for k in range(C):
                        for part in (w_hi, w_lo):
                            mm = pe.matmul(logit[0][:, 0:D], cols[:, 2, k:k + 1].to_broadcast([P, P]),
                                           part[:, WF, k, :].bitcast(F32), start=(k == 0 and part is w_hi),
                                           stop=(k == C - 1 and part is w_lo))
                    mm.then_inc(bv_made, 1)

                def hidden(g):
                    pe.wait_ge(x1lo_set, 2 * pb + g + 1)
                    ring_wait(pe, f"h{g}", t, static)
                    rows_by_weight(f"h{g}", lambda k: x1T_hi[:, g, k, :], lambda k: x1T_lo[:, g, k, :], WH)\
                        .then_inc(h_made, 1)

                def gate_logit(g):
                    ring_wait(pe, f"g{g}", t, static)
                    rows_by_weight(f"g{g}", lambda k: x1T_hi[:, g, k, :], lambda k: x1T_lo[:, g, k, :], WG)\
                        .then_inc(g_made, 1)

                def scores(g, half):
                    if (g, half) == (0, 0):
                        pe.wait_ge(maska_set, pa + 1)
                        pe.wait_ge(q_set, 3 * pa + 3)
                        pe.wait_ge(k_set, 3 * pa + 3)
                    ring_wait(pe, f"s{g}{half}", t, static)
                    bank = ring_bank(f"s{g}{half}")[:, 0:G0 * P]
                    pe.matmul(bank.rearrange("p (h m) -> p h m", h=G0), idh[:],
                              mask_a[:, g:g + 1, :].to_broadcast([P, G0, P]), start=True, stop=False,
                              skip_group_check=True)
                    feats = slice(half * DH0, (half + 1) * DH0)
                    for k in range(G0):
                        mm = pe.matmul(bank[:, k * P:(k + 1) * P], qT[feats, k, g, :], kT[feats, k, g, :],
                                       start=False, stop=(k == G0 - 1), skip_group_check=True)
                    mm.then_inc(s_made, 1)

                def transpose_probs(g, half):
                    pe.wait_ge(norm_set, 4 * pa + 2 * g + half + 1)
                    ring_wait(pe, f"pT{g}{half}", t, static)
                    for k in range(G0):
                        mm = pe.transpose(ring_bank(f"pT{g}{half}")[:, k * P:(k + 1) * P], prob[:, g, half * G0 + k, :], idf[:])
                    mm.then_inc(pT_made, 1)

                def transpose_terms():
                    pe.wait_ge(part_set, 3 * pb + 3)
                    ring_wait(pe, "sdT", t, static)
                    for g in range(PAIR):
                        mm = pe.transpose(ring_bank("sdT")[0:ROWS, g * (P // 2):(g + 1) * (P // 2)].bitcast(BF16),
                                          sd_parts[:, g, :, :].rearrange("p a s -> p (a s)"), idh[:])
                    mm.then_inc(sdT_made, 1)

                def logits(g):
                    if g == 0:
                        pe.wait_ge(maskb_set, pb + 1)
                        if static == NP and pb == 0:
                            pe.wait_ge(bf_set, 1)
                    for j in range(NZ):
                        logit_wait(pe, "z", g, j, t, static)
                        pe.matmul(logit_bank("z", g, j)[:].rearrange("p (h m) -> p h m", h=G1), idh[:],
                                  mask_b[:, g:g + 1, :].to_broadcast([P, G1, P]), start=True, stop=False,
                                  skip_group_check=True)
                    if g == 0:
                        pe.wait_ge(sdT_set, pb + 1)
                    for j in range(NZ):
                        flat = logit_bank("z", g, j)[:]
                        pe.matmul(flat, sdT[:, g, :], picks[:, G1 * j:G1 * j + G1, :].rearrange("p h m -> p (h m)"),
                                  start=False, stop=False, skip_group_check=True)
                        for k in range(G1):
                            mm = pe.matmul(flat[:, k * P:(k + 1) * P], pickd[:, G1 * j + k, :], sdT[:, g, :], start=False,
                                           stop=(k == G1 - 1), skip_group_check=True)
                        mm.then_inc(z_made, 1)

                def transpose_attention(g):
                    for j in range(NZ):
                        pe.wait_ge(att_set, 6 * pc + 3 * g + j + 1)
                        logit_wait(pe, "aT", g, j, t, static)
                        for k in range(G1):
                            mm = pe.transpose(logit_bank("aT", g, j)[:, k * P:(k + 1) * P], att[:, g, G1 * j + k, :], idf[:])
                        mm.then_inc(aT_made, 1)

                def aggregate(g):
                    ring_wait(pe, f"agg{g}", t, static)
                    bank = ring_bank(f"agg{g}")
                    for n in range(HEADS1):
                        j, k = divmod(n, G1)
                        if k == 0:
                            pe.wait_ge(aT_set, 6 * pc + 3 * g + j + 1)
                        mm = pe.matmul(bank[DH1 * k:DH1 * (k + 1), j * P:(j + 1) * P], h[:, g, n * DH1:(n + 1) * DH1],
                                       attT[:, g, n, :], start=True, stop=True)
                    mm.then_inc(agg_made, 1)

                def transpose_sums(g):
                    pe.wait_ge(aggT_set, 2 * pc + g + 1)
                    ring_wait(pe, f"f{g}", t, static)
                    for j in range(C):
                        mm = pe.transpose(ring_bank(f"f{g}")[:, j * P:(j + 1) * P], aggT[:, g, j, :], idf[:])
                    mm.then_inc(f_made, 1)

                if a:
                    qk(0)
                if b:
                    context(0)
                    context(1)
                if a:
                    qk(1)
                if b:
                    out_projection(0)
                    out_projection(1)
                if c:
                    transpose_attention(0)
                if a:
                    qk(2)
                if b:
                    transpose_x1(0)
                    transpose_x1(1)
                if c:
                    aggregate(0)
                if a:
                    scores(0, 0)
                    scores(0, 1)
                if static == NP and t == 0:
                    project_value_bias()
                if b:
                    hidden(0)
                if c:
                    transpose_sums(0)
                    transpose_attention(1)
                if b:
                    gate_logit(0)
                if c:
                    aggregate(1)
                if b:
                    hidden(1)
                if a:
                    scores(1, 0)
                    scores(1, 1)
                if c:
                    transpose_sums(1)
                if a:
                    value(0)
                    transpose_probs(0, 0)
                    transpose_probs(0, 1)
                    value(1)
                if b:
                    transpose_terms()
                    logits(0)
                    gate_logit(1)
                if a:
                    transpose_probs(1, 0)
                    transpose_probs(1, 1)
                if b:
                    logits(1)

            pe.wait_ge(const_in, 16 * N_CONST)
            run_ticks(pe, tick)

        @block.scalar
        def _(act):
            def tick(t, static, a, b, c, d):
                pa, pb, pc, pd = t, t - 1, t - 2, t - 3

                def round_context(g):
                    act.wait_ge(ctx_made, 2 * pb + g + 1)
                    act.activation(ctxT_hi[:, g, :, :].rearrange("p c n -> p (c n)"), ring_bank(f"ctx{g}")[:, 0:D],
                                   ACT.Copy).then_inc(chi_set, 1)

                def query(k):
                    act.wait_ge(qk_made, 3 * pa + k + 1)
                    act.activation(qT[:, k, :, :].rearrange("p g n -> p (g n)"), ring_bank(f"qk{k}")[:, 0:PAIR * P],
                                   ACT.Identity, bias=cols[:, 0, k:k + 1], scale=Q_SCALE)\
                        .then_inc(q_set, 1)

                def attention_exp(g, j):
                    act.wait_ge(leaky_set, 6 * pc + 3 * g + j + 1)
                    for n in range(G1 * j, G1 * j + G1):
                        op = act.activation(att[:, g, n, :], att[:, g, n, :], ACT.Exp, scale=-1.0,
                                            bias=att_min[:, g, n:n + 1], accum_out=att_sum[:, g, n:n + 1])
                    op.then_inc(att_set, 1)

                def keep_attT(g):
                    for j in range(NZ):
                        act.wait_ge(aT_made, 6 * pc + 3 * g + j + 1)
                        act.activation(attT[:, g, G1 * j:G1 * j + G1, :].rearrange("p h n -> p (h n)"),
                                       logit_bank("aT", g, j)[:], ACT.Copy).then_inc(aT_set, 1)

                def keep_sums(g):
                    act.wait_ge(agg_made, 2 * pc + g + 1)
                    act.activation(aggT[:, g, :, :].rearrange("p c n -> p (c n)"), ring_bank(f"agg{g}")[:, 0:D],
                                   ACT.Copy).then_inc(aggT_set, 1)

                def keep_probT(g, half):
                    act.wait_ge(pT_made, 4 * pa + 2 * g + half + 1)
                    act.activation(probT[:, g, half * G0:(half + 1) * G0, :].rearrange("p h n -> p (h n)"),
                                   ring_bank(f"pT{g}{half}")[:, 0:G0 * P], ACT.Copy).then_inc(pT_set, 1)

                def keep_value(g):
                    act.wait_ge(v_made, 2 * pa + g + 1)
                    act.activation(v[:, g, :], ring_bank(f"v{g}")[:, 0:D], ACT.Copy).then_inc(v_set, 1)

                def round_x1(g):
                    act.wait_ge(x1T_made, 2 * pb + g + 1)
                    act.activation(x1T_hi[:, g, :, :].rearrange("p c n -> p (c n)"), ring_bank(f"x1T{g}")[:, 0:D],
                                   ACT.Copy).then_inc(x1hi_set, 1)

                def elu_exp(g):
                    act.wait_ge(fneg_set, 2 * pc + g + 1)
                    act.activation(gated[:, g, :], gated[:, g, :], ACT.Exp).then_inc(fexp_set, 1)

                def tanh_hidden(g):
                    act.wait_ge(h_made, 2 * pb + g + 1)
                    act.activation(th[:, g, :], ring_bank(f"h{g}")[:, 0:D], ACT.Tanh).then_inc(th_set, 1)

                def tanh_gate(g):
                    act.wait_ge(gpre_set, 2 * pb + g + 1)
                    act.activation(g_tanh[:, g, :], g_tanh[:, g, :], ACT.Tanh, scale=0.5).then_inc(gtanh_set, 1)

                def score_exp(g, half):
                    act.wait_ge(max_set, 4 * pa + 2 * g + half + 1)
                    for k in range(G0):
                        n = half * G0 + k
                        op = act.activation(prob[:, g, n, :], ring_bank(f"s{g}{half}")[:, k * P:(k + 1) * P], ACT.Exp,
                                            bias=neg_max[:, g, n:n + 1], accum_out=p_sum[:, g, n:n + 1])
                    op.then_inc(prob_set, 1)

                def relu_logits(g, j):
                    act.wait_ge(z_made, 6 * pb + 3 * g + j + 1)
                    act.activation(att[:, g, G1 * j:G1 * j + G1, :].rearrange("p h m -> p (h m)"),
                                   logit_bank("z", g, j)[:], ACT.Relu, scale=1.0 / SLOPE - 1.0).then_inc(relu_set[g], 1)

                if c:
                    attention_exp(0, 0)
                if a:
                    query(0)
                if b:
                    round_context(0)
                    round_context(1)
                if c:
                    attention_exp(0, 1)
                if a:
                    query(1)
                if c:
                    attention_exp(0, 2)
                    attention_exp(1, 0)
                    attention_exp(1, 1)
                    keep_attT(0)
                if a:
                    query(2)
                if b:
                    round_x1(0)
                    round_x1(1)
                if c:
                    attention_exp(1, 2)
                    keep_sums(0)
                if a:
                    score_exp(0, 0)
                if b:
                    tanh_hidden(0)
                if a:
                    score_exp(0, 1)
                if c:
                    keep_attT(1)
                    elu_exp(0)
                    keep_sums(1)
                if b:
                    tanh_gate(0)
                    tanh_hidden(1)
                if a:
                    score_exp(1, 0)
                    score_exp(1, 1)
                    keep_value(0)
                if c:
                    elu_exp(1)
                if a:
                    keep_probT(0, 0)
                    keep_probT(0, 1)
                    keep_value(1)
                if b:
                    for j in range(NZ):
                        relu_logits(0, j)
                if a:
                    keep_probT(1, 0)
                    keep_probT(1, 1)
                if b:
                    tanh_gate(1)
                    for j in range(NZ):
                        relu_logits(1, j)

            act.wait_ge(bq_scaled, 1)
            run_ticks(act, tick)

        @block.vector
        def _(dve):
            def round_x(g, pair):
                if g == 0:
                    dve.wait_ge(xT_loaded, 16 * pair + 16)
                dve.tensor_copy(xT_hi[:, :, g, :], xT_in[:, :, g, :]).then_inc(xhi_set, 1)

            def carried_wait(s, value):
                dve.wait_ge(bq_scaled, 1)
                dve.wait_ge(s, value)

            round_x(0, 0)
            round_x(1, 0)
            for n in range(6):
                dve.wait_ge(w_in, 16 * n + 16)
                dve.tensor_copy(w_hi[:, n, :, :], w_f32[:]).then_inc(w_rounded, 1)
                dve.wait_ge(w_rounded, n + 1)
                dve.tensor_tensor(w_lo[:, n, :, :], w_f32[:], w_hi[:, n, :, :].bitcast(F32), ALU.subtract)\
                    .then_inc(w_split, 1)
                if n == 1:
                    dve.wait_ge(const_in, 16 * N_CONST)
                    dve.tensor_scalar(cols[:, 0, :], cols[:, 0, :], Q_SCALE, None, ALU.mult).then_inc(bq_scaled, 1)

            def tick(t, static, a, b, c, d):
                pa, pb, pc, pd = t, t - 1, t - 2, t - 3

                def keep_mask():
                    if static is None or pb > 0:
                        dve.wait_ge(z_made, 6 * pb)
                    dve.wait_ge(maska_set, pb + 1)
                    dve.tensor_copy(mask_b[:], mask_a[:]).then_inc(maskb_set, 1)

                def make_mask():
                    dve.wait_ge(adj_loaded, 16 * pa + 16)
                    if static is None or pa > 0:
                        dve.wait_ge(s_made, 4 * pa)
                        dve.wait_ge(maskb_set, pa)
                    dve.tensor_scalar(mask_a[:], adj_in[:], -1.0, -MASKED, ALU.add, ALU.mult).then_inc(maska_set, 1)

                def rest_context(g):
                    dve.wait_ge(chi_set, 2 * pb + g + 1)
                    dve.tensor_tensor(ctxT_lo[:, g, :, :].rearrange("p c n -> p (c n)"), ring_bank(f"ctx{g}")[:, 0:D],
                                      ctxT_hi[:, g, :, :].rearrange("p c n -> p (c n)").bitcast(F32), ALU.subtract)\
                       .then_inc(clo_set, 1)

                def key(k):
                    dve.wait_ge(q_set, C * pa + k + 1)
                    dve.tensor_scalar(kT[:, k, :, :].rearrange("p g n -> p (g n)"), ring_bank(f"qk{k}")[:, PAIR * P:2 * PAIR * P],
                                      cols[:, 1, k:k + 1], None, ALU.add).then_inc(k_set, 1)

                def residual(g):
                    dve.wait_ge(out_made, 2 * pb + g + 1)
                    dve.wait_ge(xres_set, 2 * pb + g + 1)
                    dve.tensor_tensor(x1[:, g, :], ring_bank(f"out{g}")[:, 0:D], x_res[:, g, :], ALU.add).then_inc(y0_set, 1)
                    dve.wait_ge(y0_set, 2 * pb + g + 1)
                    dve.bn_stats(stats0[:, g, :], x1[:, g, :]).then_inc(st0_set, 1)

                def aggregate0(g):
                    carried_wait(st0_set, 2 * pb + g + 1)
                    dve.bn_aggr(mv0[:, g, :], stats0[:, g, :]).then_inc(mv0_set, 1)

                def normalize0(g):
                    dve.wait_ge(rstd0_set, 2 * pb + g + 1)
                    dve.tensor_scalar(x1[:, g, :], x1[:, g, :], mv0[:, g, 0:1], rstd0[:, g:g + 1], ALU.subtract, ALU.mult)\
                       .then_inc(x1_set, 1)

                def rest_x1(g):
                    dve.wait_ge(x1hi_set, 2 * pb + g + 1)
                    dve.tensor_tensor(x1T_lo[:, g, :, :].rearrange("p c n -> p (c n)"), ring_bank(f"x1T{g}")[:, 0:D],
                                      x1T_hi[:, g, :, :].rearrange("p c n -> p (c n)").bitcast(F32), ALU.subtract)\
                       .then_inc(x1lo_set, 1)

                def hidden(g):
                    dve.wait_ge(th_set, 2 * pb + g + 1)
                    if static is None or pb > 0:
                        dve.wait_ge(agg_made, 2 * (pb - 1) + g + 1)
                    dve.tensor_tensor(h[:, g, :], ring_bank(f"h{g}")[:, 0:D], rows[:, BH, :], ALU.add).then_inc(h_set, 1)

                def add_value_bias():
                    dve.wait_ge(bv_made, 1)
                    dve.tensor_tensor(rows[:, BF, :], logit[0][:, 0:D], rows[:, BF, :], ALU.add).then_inc(bf_set, 1)

                def gate_bias(g):
                    dve.wait_ge(g_made, 2 * pb + g + 1)
                    dve.tensor_tensor(g_tanh[:, g, :], ring_bank(f"g{g}")[:, 0:D], rows[:, BG, :], ALU.add).then_inc(gpre_set, 1)

                def score_max(g, half):
                    dve.wait_ge(s_made, 4 * pa + 2 * g + half + 1)
                    dve.tensor_reduce(neg_max[:, g, half * G0:(half + 1) * G0],
                                      ring_bank(f"s{g}{half}")[:, 0:G0 * P].rearrange("p (h m) -> p h m", h=G0),
                                      AX.X, ALU.max, negate=True).then_inc(max_set, 1)

                def invert_sum(g, half):
                    dve.wait_ge(prob_set, 4 * pa + 2 * g + half + 1)
                    heads = slice(half * G0, (half + 1) * G0)
                    dve.reciprocal(p_inv[:, g, heads], p_sum[:, g, heads]).then_inc(inv_set, 1)

                def logit_terms(g):
                    dve.wait_ge(thw_set, 2 * pb + g + 1)
                    dve.tensor_reduce(terms[:, g, :], th_w[:, g, :, :].rearrange("p s (h e) -> p (s h) e", e=DH1),
                                      AX.X, ALU.add).then_inc(terms_set, 1)

                def split_terms():
                    dve.wait_ge(terms_set, 2 * pb + 2)
                    dve.tensor_copy(sd_parts[:, :, 0, :], terms[:]).then_inc(part_set, 1)
                    dve.wait_ge(part_set, 3 * pb + 1)
                    dve.tensor_tensor(sd_rest[:], terms[:], sd_parts[:, :, 0, :], ALU.subtract).then_inc(rest_set, 1)
                    dve.wait_ge(rest_set, 2 * pb + 1)
                    dve.tensor_copy(sd_parts[:, :, 1, :], sd_rest[:]).then_inc(part_set, 1)
                    dve.wait_ge(part_set, 3 * pb + 2)
                    dve.tensor_tensor(sd_rest2[:], sd_rest[:], sd_parts[:, :, 1, :], ALU.subtract).then_inc(rest_set, 1)
                    dve.wait_ge(rest_set, 2 * pb + 2)
                    dve.tensor_copy(sd_parts[:, :, 2, :], sd_rest2[:]).then_inc(part_set, 1)

                def keep_terms():
                    dve.wait_ge(sdT_made, pb + 1)
                    dve.tensor_copy(sdT[:].rearrange("p g n -> p (g n)"),
                                    ring_bank("sdT")[0:ROWS, 0:PAIR * P // 2].bitcast(BF16)).then_inc(sdT_set, 1)

                def leaky(g, j):
                    carried_wait(relu_set[g], NZ * pb + j + 1 if j < NZ - 1 else NZ * pa)
                    for n in range(G1 * j, G1 * j + G1):
                        op = dve.tensor_tensor_reduce(
                            out=att[:, g, n, :], in0=logit_bank("z", g, j)[:, (n - G1 * j) * P:(n - G1 * j + 1) * P],
                            in1=att[:, g, n, :], scale=-SLOPE, scalar=3.0e38, op0=ALU.add, op1=ALU.min,
                            accum_out=att_min[:, g, n:n + 1])
                    op.then_inc(leaky_set, 1)

                def weigh(g):
                    dve.wait_ge(att_set, 6 * pc + 3 * g + 3)
                    dve.reciprocal(a_inv[:, g, :], att_sum[:, g, :]).then_inc(ainv_set, 1)
                    dve.wait_ge(ainv_set, 2 * pc + g + 1)
                    dve.wait_ge(f_made, 2 * pc + g + 1)
                    dve.tensor_tensor(f[:, g, :].rearrange("p (h e) -> p h e", h=HEADS1),
                                      ring_bank(f"f{g}")[:, 0:D].rearrange("p (h e) -> p h e", h=HEADS1),
                                      a_inv[:, g, :].unsqueeze(2).to_broadcast([P, HEADS1, DH1]), ALU.mult).then_inc(f_set, 1)
                    dve.wait_ge(f_set, 2 * pc + g + 1)
                    dve.tensor_scalar(gated[:, g, :], f[:, g, :], 0.0, None, ALU.min).then_inc(fneg_set, 1)

                def elu_and_gate(g):
                    dve.wait_ge(fexp_set, 2 * pc + g + 1)
                    dve.scalar_tensor_tensor(out=gated[:, g, :], in0=f[:, g, :], scalar=0.0, in1=gated[:, g, :],
                                             op0=ALU.max, op1=ALU.add).then_inc(elu_set, 1)
                    dve.wait_ge(elu_set, 2 * pc + g + 1)
                    dve.wait_ge(gate_set, 2 * pc + g + 1)
                    dve.scalar_tensor_tensor(out=gated[:, g, :], in0=gated[:, g, :], scalar=-1.0, in1=gate[:, g, :],
                                             op0=ALU.add, op1=ALU.mult).then_inc(gated_set, 1)

                def ungated(g):
                    dve.wait_ge(gate_set, 2 * pb + g + 1)
                    if static is None or pb > 0:
                        dve.wait_ge(y1_set, 2 * (pb - 1) + g + 1)
                    dve.scalar_tensor_tensor(out=gx[:, g, :], in0=gate[:, g, :], scalar=-2.0, in1=x1[:, g, :],
                                             op0=ALU.add, op1=ALU.mult).then_inc(gx_set, 1)

                def moments1(g):
                    dve.wait_ge(y1_set, 2 * pd + g + 1)
                    dve.bn_stats(stats1[:, g, :], y1[:, g, :]).then_inc(st1_set, 1)

                def aggregate1(g):
                    carried_wait(st1_set, 2 * pd + g + 1)
                    dve.bn_aggr(mv1[:, g, :], stats1[:, g, :]).then_inc(mv1_set, 1)

                def normalize1(g):
                    if g == 0 and (static is None or pd > 0):
                        dve.wait_ge(stored, 16 * pd)
                    dve.wait_ge(rstd1_set, 2 * pd + g + 1)
                    dve.tensor_scalar(y_out[:, g, :], y1[:, g, :], mv1[:, g, 0:1], rstd1[:, g:g + 1], ALU.subtract, ALU.mult)\
                       .then_inc(yout_set, 1)

                if a:
                    key(0)
                if b:
                    rest_context(0)
                    rest_context(1)
                    keep_mask()
                if a:
                    make_mask()
                    key(1)
                if b:
                    residual(0)
                    aggregate0(0)
                    residual(1)
                    aggregate0(1)
                    normalize0(0)
                    normalize0(1)
                if a:
                    key(2)
                if b:
                    rest_x1(0)
                    rest_x1(1)
                if d:
                    moments1(0)
                if a:
                    score_max(0, 0)
                if d:
                    moments1(1)
                if a:
                    score_max(0, 1)
                if static == NP and t == 0:
                    add_value_bias()
                if d:
                    aggregate1(0)
                    aggregate1(1)
                if b:
                    hidden(0)
                if c:
                    weigh(0)
                if a:
                    invert_sum(0, 0)
                    invert_sum(0, 1)
                if d:
                    normalize1(0)
                    normalize1(1)
                if b:
                    gate_bias(0)
                if c:
                    elu_and_gate(0)
                if b:
                    logit_terms(0)
                if a:
                    score_max(1, 0)
                if b:
                    hidden(1)
                if a:
                    score_max(1, 1)
                if c:
                    weigh(1)
                if b:
                    logit_terms(1)
                    split_terms()
                if a:
                    invert_sum(1, 0)
                    invert_sum(1, 1)
                if b:
                    keep_terms()
                if static is None or t + 1 < NP:
                    dve.wait_ge(v_made, 2 * t + 2)
                    round_x(0, t + 1)
                    round_x(1, t + 1)
                if c:
                    elu_and_gate(1)
                if b:
                    leaky(0, 0)
                    leaky(0, 1)
                    gate_bias(1)
                    leaky(0, 2)
                    ungated(0)
                    leaky(1, 0)
                    leaky(1, 1)
                    ungated(1)
                    leaky(1, 2)

            run_ticks(dve, tick)

        @block.gpsimd
        def _(pool):
            def rest_x(g, pair):
                pool.wait_ge(xhi_set, 2 * pair + g + 1)
                pool.tensor_tensor(xT_lo[:, :, g, :], xT_in[:, :, g, :], xT_hi[:, :, g, :].bitcast(F32),
                                   ALU.subtract).then_inc(xlo_set, 1)

            def tick(t, static, a, b, c, d):
                pa, pb, pc, pd = t, t - 1, t - 2, t - 3

                def residual_input(g):
                    if g == 0 and static == NP and pa == 0:
                        pool.wait_ge(bf_set, 1)
                    if g == 0:
                        pool.wait_ge(x_loaded, 16 * pa + 16)
                    if static is None or pa > 0:
                        pool.wait_ge(y0_set, 2 * (pa - 1) + g + 1)
                    pool.tensor_tensor(x_res[:, g, :], x_in[:, g, :], rows[:, BF, :], ALU.add).then_inc(xres_set, 1)

                def inverse_deviation(g, mv, ve, rstd, mv_set, ve_set, rstd_set, pair):
                    pool.wait_ge(mv_set, 2 * pair + g + 1)
                    pool.tensor_tensor(ve[:, g:g + 1], mv[:, g, 1:2], eps[:], ALU.add).then_inc(ve_set, 1)
                    pool.wait_ge(ve_set, 2 * pair + g + 1)
                    pool.tensor_tensor(rstd[:, g:g + 1], ve[:, g:g + 1], neg_half[:], ALU.pow).then_inc(rstd_set, 1)

                def gated_sum(g):
                    pool.wait_ge(gated_set, 2 * pc + g + 1)
                    pool.wait_ge(gx_set, 2 * pc + g + 1)
                    pool.tensor_tensor(y1[:, g, :], gated[:, g, :], gx[:, g, :], ALU.subtract).then_inc(y1_set, 1)

                def normalize_probs(g, half):
                    pool.wait_ge(inv_set, 4 * pa + 2 * g + half + 1)
                    heads = slice(half * G0, (half + 1) * G0)
                    pool.tensor_tensor(prob[:, g, heads, :], prob[:, g, heads, :],
                                       p_inv[:, g, heads].unsqueeze(2).to_broadcast([P, G0, P]), ALU.mult).then_inc(norm_set, 1)

                def gate_value(g):
                    pool.wait_ge(half_set, 2)
                    pool.wait_ge(gtanh_set, 2 * pb + g + 1)
                    if static is None or pb > 0:
                        pool.wait_ge(gated_set, 2 * pc + g + 1)
                    pool.tensor_scalar(gate[:, g, :], g_tanh[:, g, :], 0.5, 0.5, ALU.mult, ALU.add).then_inc(gate_set, 1)

                def weigh_hidden(g):
                    pool.wait_ge(th_set, 2 * pb + g + 1)
                    pool.tensor_tensor(th_w[:, g, :, :], th[:, g:g + 1, :].to_broadcast([P, 2, D]),
                                       rows[:, W_SRC:W_DST + 1, :], ALU.mult).then_inc(thw_set, 1)

                if b:
                    inverse_deviation(0, mv0, ve0, rstd0, mv0_set, ve0_set, rstd0_set, pb)
                    inverse_deviation(1, mv0, ve0, rstd0, mv0_set, ve0_set, rstd0_set, pb)
                if a:
                    residual_input(0)
                    residual_input(1)
                if d:
                    inverse_deviation(0, mv1, ve1, rstd1, mv1_set, ve1_set, rstd1_set, pd)
                    inverse_deviation(1, mv1, ve1, rstd1, mv1_set, ve1_set, rstd1_set, pd)
                if b:
                    weigh_hidden(0)
                if a:
                    normalize_probs(0, 0)
                    normalize_probs(0, 1)
                if c:
                    gated_sum(0)
                if b:
                    weigh_hidden(1)
                if a:
                    normalize_probs(1, 0)
                    normalize_probs(1, 1)
                if b:
                    gate_value(0)
                if c:
                    gated_sum(1)
                if static is None or t + 1 < NP:
                    rest_x(0, t + 1)
                    rest_x(1, t + 1)
                if b:
                    gate_value(1)

            pool.memset(neg_half[:], -0.5).then_inc(half_set, 1)
            pool.memset(eps[:], EPS).then_inc(half_set, 1)
            pool.wait_ge(half_set, 2)
            rest_x(0, 0)
            rest_x(1, 0)
            run_ticks(pool, tick)


def kernel(**inputs):
    import concourse.bacc as bacc
    import ml_dtypes
    import numpy as np
    from concourse.bass_utils import run_bass_kernel_spmd

    def arr(name):
        return np.asarray(inputs[name])

    def by_partition(w):
        return w.reshape(-1, P, w.shape[-1]).transpose(1, 0, 2)

    x, adj = arr("x"), arr("adj")
    D = x.shape[-1]
    W, w_src, w_dst = arr("L1_gnn_W"), arr("L1_gnn_w_src"), arr("L1_gnn_w_dst")
    heads = W.shape[0]
    row = np.arange(PARTS * 2 * heads) % (2 * heads)
    pick = (row[:, None] == np.arange(2 * heads)[None, :])[:, :, None] & np.ones(P, bool)
    arrays = {
        "x": x,
        "xT": x.reshape(-1, PAIR, P, D // P, P).transpose(0, 4, 3, 1, 2),
        "adj": adj.transpose(1, 0, 2),
        "weights": np.stack([by_partition(w) for w in (
            arr("L0_gnn_Wq"), arr("L0_gnn_Wk"), arr("L0_gnn_Wv"), arr("L0_gnn_Wf"),
            W.transpose(1, 0, 2).reshape(D, -1), arr("L1_gnn_H_w").T)]),
        "bias_rows": np.stack([np.broadcast_to(b, (P, D)) for b in (
            arr("L0_gnn_bf"), np.tile(arr("L1_gnn_b"), heads), arr("L1_gnn_H_b"),
            w_src.reshape(D), w_dst.reshape(D))], axis=1),
        "bias_cols": np.stack([arr(n).reshape(-1, P).T for n in ("L0_gnn_bq", "L0_gnn_bk", "L0_gnn_bv")], axis=1),
        "ident": np.eye(P, dtype=np.float32),
        "ident_h": np.eye(P, dtype=ml_dtypes.bfloat16),
        "pick_s": pick[:, :heads].astype(ml_dtypes.bfloat16),
        "pick_d": pick[:, heads:].astype(ml_dtypes.bfloat16),
    }
    arrays = {n: np.ascontiguousarray(a) for n, a in arrays.items()}
    nc = bacc.Bacc("TRN2", target_bir_lowering=False, num_devices=1)
    args = [nc.dram_tensor(n, a.shape, mybir.dt.from_np(a.dtype), kind="ExternalInput").ap() for n, a in arrays.items()]
    out = nc.dram_tensor("out", x.shape, F32, kind="ExternalOutput").ap()
    build(nc, *args, out)
    result = run_bass_kernel_spmd(nc, [arrays], core_ids=[0])
    return result.results[0]["out"]
```

```python
from contextlib import ExitStack

import concourse.bass as bass
from concourse import mybir

F32 = mybir.dt.float32
F32R = mybir.dt.float32r
BF16 = mybir.dt.bfloat16
U8 = mybir.dt.uint8
ALU = mybir.AluOpType
ACT = mybir.ActivationFunctionType
AX = mybir.AxisListType

P = 128
PAIR = 2
HEADS0 = 6
HEADS1 = 12
PARTS = 3
MASKED = -9.0e15
EPS = 1e-5
SLOPE = 0.2

RING = 4
JOBS = [
    ("qk0", "A"), ("ctx0", "B"), ("ctx1", "B"), ("qk1", "A"), ("out0", "B"), ("out1", "B"),
    ("qk2", "A"), ("x1T0", "B"), ("x1T1", "B"), ("agg0", "C"), ("s00", "A"), ("s01", "A"),
    ("h0", "B"), ("f0", "C"), ("g0", "B"), ("agg1", "C"), ("h1", "B"), ("s10", "A"),
    ("s11", "A"), ("f1", "C"), ("v0", "A"), ("pT00", "A"), ("pT01", "A"), ("v1", "A"),
    ("termsT", "B"), ("pT10", "A"), ("pT11", "A"), ("g1", "B"),
]
SLOT = {name: k for k, (name, _) in enumerate(JOBS)}
RING1 = 4
JOBS1 = [(f"{kind}{g}{j}", stage) for kind, stage in (("aT", "C"), ("z", "B")) for g in range(2) for j in range(3)]
SLOT1 = {name: k for k, (name, _) in enumerate(JOBS1)}
LAG = {"A": 0, "B": 1, "C": 2}


def tenant_before(jobs, name, tick, pairs):
    at = [n for n, _ in jobs].index(name)
    if pairs is None:
        n, stage = jobs[at - 1]
        return n, tick - LAG[stage] - (at == 0)
    earlier = [(tick, job) for job in jobs[:at]]
    for back in range(1, 4):
        earlier = [(tick - back, job) for job in jobs] + earlier
    for at_tick, (n, stage) in reversed(earlier):
        if 0 <= at_tick - LAG[stage] < pairs:
            return n, at_tick - LAG[stage]
    return None


def build(nc, x, xT, adj, weights, bias_rows, bias_cols, ident, ident_h, pick, out):
    B, _, D = x.shape
    C = D // P
    DH0 = D // HEADS0
    DH1 = D // HEADS1
    NP = B // PAIR
    G0 = HEADS0 // 2
    G1 = 4
    NZ = HEADS1 // G1
    KINDS = 3
    ROWS = KINDS * PARTS * HEADS1
    Q_SCALE = float(DH0) ** -0.5
    WQ, WK, WV, WF, WH, WG = range(6)
    BF, BH, BG, W_DST, W_SRC = range(5)
    assert NP > 5 and C * P == D and NZ == 3

    with ExitStack() as ctx:
        def sb(name, shape, dt=F32):
            return ctx.enter_context(nc.sbuf_tensor(name, shape, dt))

        def sem(name):
            return ctx.enter_context(nc.semaphore(name))

        ring = [ctx.enter_context(nc.psum_tensor(f"ring{k}", [P, 512], F32)) for k in range(RING)]
        logit = [ctx.enter_context(nc.psum_tensor(f"logit{k}", [P, 512], F32)) for k in range(RING1)]

        w_hi = sb("w_hi", [P, 6, C, D], F32R)
        w_lo = sb("w_lo", [P, 6, C, D], F32R)
        rows = sb("rows", [P, 5, D])
        cols = sb("cols", [P, 3, C])
        idf = sb("idf", [P, P])
        idh = sb("idh", [P, P], BF16)
        picks = sb("picks", [ROWS, KINDS, HEADS1, P], BF16)
        neg_half = sb("neg_half", [P, 1])
        eps = sb("eps", [P, 1])
        xT_in = sb("xT_in", [P, C, PAIR, P])
        x_in = sb("x_in", [P, PAIR, D])
        adj_in = sb("adj_in", [P, PAIR, P], U8)
        mask_a = sb("mask_a", [P, PAIR, P], BF16)
        x_res = sb("x_res", [P, PAIR, D])
        xT_hi = sb("xT_hi", [P, C, PAIR, P], F32R)
        xT_lo = sb("xT_lo", [P, C, PAIR, P], F32R)
        qT = sb("qT", [P, C, PAIR, P])
        kT = sb("kT", [P, C, PAIR, P])
        v = sb("v", [P, PAIR, D])
        neg_max = sb("neg_max", [P, PAIR, HEADS0])
        p_sum = sb("p_sum", [P, PAIR, HEADS0])
        p_inv = sb("p_inv", [P, PAIR, HEADS0])
        prob = sb("prob", [P, PAIR, HEADS0, P])
        probT = sb("probT", [P, PAIR, HEADS0, P])
        mask_b = sb("mask_b", [P, PAIR, P], BF16)
        ctxT_hi = sb("ctxT_hi", [P, PAIR, C, P], F32R)
        ctxT_lo = sb("ctxT_lo", [P, PAIR, C, P], F32R)
        x1 = sb("x1", [P, PAIR, D])
        stats0 = sb("stats0", [P, PAIR, 6])
        mv0 = sb("mv0", [P, PAIR, 2])
        ve0 = sb("ve0", [P, PAIR])
        rstd0 = sb("rstd0", [P, PAIR])
        x1T_hi = sb("x1T_hi", [P, PAIR, C, P], F32R)
        x1T_lo = sb("x1T_lo", [P, PAIR, C, P], F32R)
        h = sb("h", [P, PAIR, D])
        th = sb("th", [P, PAIR, D])
        th_w = sb("th_w", [P, PAIR, 2, D])
        terms = sb("terms", [P, PAIR, 2, HEADS1])
        source = sb("source", [P, HEADS1])
        g_tanh = sb("g_tanh", [P, PAIR, D])
        gate = sb("gate", [P, PAIR, D])
        gx = sb("gx", [P, PAIR, D])
        parts = sb("parts", [P, KINDS, PARTS, HEADS1], BF16)
        rest = sb("rest", [P, KINDS, HEADS1])
        rest2 = sb("rest2", [P, KINDS, HEADS1])
        termsT = sb("termsT", [ROWS, P], BF16)
        att = sb("att", [P, PAIR, HEADS1, P])
        att_min = sb("att_min", [P, PAIR, HEADS1])
        att_sum = sb("att_sum", [P, PAIR, HEADS1])
        attT = sb("attT", [P, PAIR, HEADS1, P])
        a_inv = sb("a_inv", [P, PAIR, HEADS1])
        aggT = sb("aggT", [P, PAIR, C, P])
        f = sb("f", [P, PAIR, D])
        gated = sb("gated", [P, PAIR, D])
        y1 = sb("y1", [P, PAIR, D])
        stats1 = sb("stats1", [P, PAIR, 6])
        mv1 = sb("mv1", [P, PAIR, 2])
        ve1 = sb("ve1", [P, PAIR])
        rstd1 = sb("rstd1", [P, PAIR])
        y_out = sb("y_out", [P, PAIR, D])

        raw_weight = [buffer.rearrange("p h n -> p (h n)")[:, 0:C * D].rearrange("p (c f) -> p c f", c=C) for buffer in (
            prob[:].rearrange("p g h n -> p (g h) n"), probT[:].rearrange("p g h n -> p (g h) n"),
            attT[:, 0, :, :], attT[:, 1, :, :], att[:, 0, :, :], att[:, 1, :, :])]

        cols_in, const_in = sem("cols_in"), sem("const_in")
        w_in = [sem(f"w{n}_in") for n in range(6)]
        w_rounded = sem("w_rounded")
        w_split = sem("w_split")
        bq_scaled = sem("bq_scaled")
        half_set = sem("half_set")
        bv_made, bf_set = sem("bv_made"), sem("bf_set")
        x_loaded = sem("x_loaded")
        xT_loaded = sem("xT_loaded")
        adj_loaded = sem("adj_loaded")
        stored = sem("stored")
        qk_made, v_made = sem("qk_made"), sem("v_made")
        s_made, pT_made, ctx_made = sem("s_made"), sem("pT_made"), sem("ctx_made")
        out_made, x1T_made, h_made = sem("out_made"), sem("x1T_made"), sem("h_made")
        g_made, termsT_made, z_made = sem("g_made"), sem("termsT_made"), sem("z_made")
        aT_made, agg_made, f_made = sem("aT_made"), sem("agg_made"), sem("f_made")
        xhi_set, xlo_set, q_set, k_set, v_set = (
            sem(n) for n in ("xhi_set", "xlo_set", "q_set", "k_set", "v_set"))
        max_set, prob_set, inv_set, norm_set, pT_set = (
            sem(n) for n in ("max_set", "prob_set", "inv_set", "norm_set", "pT_set"))
        chi_set, clo_set, y0_set, st0_set, mv0_set = (
            sem(n) for n in ("chi_set", "clo_set", "y0_set", "st0_set", "mv0_set"))
        ve0_set, rstd0_set, x1_set, x1hi_set, x1lo_set = (
            sem(n) for n in ("ve0_set", "rstd0_set", "x1_set", "x1hi_set", "x1lo_set"))
        h_set, th_set, thw_set, gpre_set, gtanh_set = (
            sem(n) for n in ("h_set", "th_set", "thw_set", "gpre_set", "gtanh_set"))
        gate_set, gx_set, terms_set, part_set, rest_set, source_set, termsT_set = (
            sem(n) for n in ("gate_set", "gx_set", "terms_set", "part_set", "rest_set", "source_set", "termsT_set"))
        relu_set = [sem(f"relu{g}_set") for g in range(PAIR)]
        masked_set = sem("masked_set")
        leaky_set, att_set = sem("leaky_set"), sem("att_set")
        aT_set, ainv_set, aggT_set, f_set, fneg_set, fexp_set = (
            sem(n) for n in ("aT_set", "ainv_set", "aggT_set", "f_set", "fneg_set", "fexp_set"))
        elu_set, gated_set, y1_set, st1_set, mv1_set = (
            sem(n) for n in ("elu_set", "gated_set", "y1_set", "st1_set", "mv1_set"))
        ve1_set, rstd1_set, yout_set = (
            sem(n) for n in ("ve1_set", "rstd1_set", "yout_set"))
        maska_set, maskb_set, xres_set = (
            sem(n) for n in ("maska_set", "maskb_set", "xres_set"))

        N_CONST = 4

        def need(eng, s, value):
            if not isinstance(value, int) or value > 0:
                eng.wait_ge(s, value)

        def run_ticks(eng, tick):
            def peeled(t):
                tick(t, NP, t < NP, 1 <= t < NP + 1, 2 <= t < NP + 2, 3 <= t)
            for t in range(4):
                peeled(t)
            with eng.Fori(4, NP - 1) as t:
                tick(t, None, True, True, True, True)
            for t in range(NP - 1, NP + 3):
                peeled(t)

        def ring_bank(name):
            return ring[SLOT[name] % RING]

        readers = {"termsT": [(termsT_set, 1, 1)]}
        for g in range(PAIR):
            readers[f"ctx{g}"] = [(clo_set, 2, g + 1)]
            readers[f"out{g}"] = [(y0_set, 2, g + 1)]
            readers[f"agg{g}"] = [(aggT_set, 2, g + 1)]
            readers[f"f{g}"] = [(f_set, 2, g + 1)]
            readers[f"x1T{g}"] = [(x1lo_set, 2, g + 1)]
            readers[f"v{g}"] = [(v_set, 2, g + 1)]
            readers[f"h{g}"] = [(h_set, 2, g + 1)]
            readers[f"g{g}"] = [(gpre_set, 2, g + 1)]
            for half in range(2):
                readers[f"s{g}{half}"] = [(prob_set, 4, 2 * g + half + 1)]
                readers[f"pT{g}{half}"] = [(pT_set, 4, 2 * g + half + 1)]
            for j in range(NZ):
                readers[f"aT{g}{j}"] = [(aT_set, 6, NZ * g + j + 1)]
                readers[f"z{g}{j}"] = [(leaky_set, 6, NZ * g + j + 1)]
        for k in range(C):
            readers[f"qk{k}"] = [(k_set, C, k + 1)]

        def wait_read(eng, tenant):
            if tenant is not None:
                name, pair = tenant
                for s, per_pair, count in readers[name]:
                    eng.wait_ge(s, per_pair * pair + count)

        def ring_wait(eng, name, t, static):
            wait_read(eng, tenant_before(JOBS[SLOT[name] % RING::RING], name, t, static))

        def logit_bank(kind, g, j):
            return logit[SLOT1[f"{kind}{g}{j}"] % RING1]

        def logit_wait(eng, kind, g, j, t, static):
            name = f"{kind}{g}{j}"
            wait_read(eng, tenant_before(JOBS1[SLOT1[name] % RING1::RING1], name, t, static))

        block = ctx.enter_context(nc.Block())

        @block.sync
        def _(sp):
            sp.dma_start(xT_in[:], xT[0]).then_inc(xT_loaded, 16)
            for n in range(6):
                sp.dma_start(raw_weight[n], weights[n]).then_inc(w_in[n], 16)
                if n == 1:
                    sp.dma_start(cols[:], bias_cols).then_inc(cols_in, 16)
                    for dst, src in ((rows[:], bias_rows), (idf[:], ident), (idh[:], ident_h),
                                     (picks[:], pick)):
                        sp.dma_start(dst, src).then_inc(const_in, 16)
                    sp.dma_start(adj_in[:], adj[:, 0:PAIR, :]).then_inc(adj_loaded, 16)
                    sp.dma_start(x_in[:], x[0:PAIR].rearrange("b n d -> n b d")).then_inc(x_loaded, 16)
            sp.wait_ge(xlo_set, 2)
            sp.dma_start(xT_in[:], xT[1]).then_inc(xT_loaded, 16)

            def tick(t, static, d):
                more, after, done = (t + 1) * PAIR, t + 2, (t - 3) * PAIR
                if static is None or t + 1 < NP:
                    sp.wait_ge(maska_set, t + 1)
                    sp.wait_ge(xres_set, 2 * t + 2)
                    sp.dma_start(x_in[:], x[bass.ds(more, PAIR)].rearrange("b n d -> n b d")).then_inc(x_loaded, 16)
                    sp.dma_start(adj_in[:], adj[:, bass.ds(more, PAIR), :]).then_inc(adj_loaded, 16)
                if static is None or t + 2 < NP:
                    sp.wait_ge(xlo_set, 2 * t + 4)
                    sp.dma_start(xT_in[:], xT[after]).then_inc(xT_loaded, 16)
                if d:
                    sp.wait_ge(yout_set, 2 * (t - 3) + 2)
                    sp.dma_start(out[bass.ds(done, PAIR)].rearrange("b n d -> n b d"), y_out[:]).then_inc(stored, 16)

            for t in range(3):
                tick(t, NP, False)
            with sp.Fori(3, NP - 2) as t:
                tick(t, None, True)
            for t in range(NP - 2, NP + 3):
                tick(t, NP, True)
            sp.wait_ge(stored, 16 * NP)

        @block.tensor
        def _(pe):
            def split_product(dst, terms):
                for n, (stationary, moving) in enumerate(terms):
                    mm = pe.matmul(dst, stationary, moving, start=(n == 0), stop=(n == len(terms) - 1))
                return mm

            def rows_by_weight(name, hiT, loT, w):
                terms = []
                for k in range(C):
                    terms += [(hiT(k), w_hi[:, w, k, :]), (hiT(k), w_lo[:, w, k, :]), (loT(k), w_hi[:, w, k, :])]
                return split_product(ring_bank(name)[:, 0:D], terms)

            def tick(t, static, a, b, c, d):
                pa, pb, pc, pd = t, t - 1, t - 2, t - 3

                def context(g):
                    pe.wait_ge(pT_set, 4 * pb + 2 * g + 2)
                    ring_wait(pe, f"ctx{g}", t, static)
                    bank = ring_bank(f"ctx{g}")
                    for k in range(C):
                        for half in range(2):
                            mm = pe.matmul(bank[DH0 * half:DH0 * half + DH0, k * P:(k + 1) * P],
                                           v[:, g, (2 * k + half) * DH0:(2 * k + half + 1) * DH0],
                                           probT[:, g, half * G0 + k, :], start=True, stop=True)
                    mm.then_inc(ctx_made, 1)

                def qk(k):
                    if k == 0:
                        pe.wait_ge(xlo_set, 2 * pa + 2)
                        if static == NP and pa == 0:
                            pe.wait_ge(w_split, 2)
                    ring_wait(pe, f"qk{k}", t, static)
                    bank = ring_bank(f"qk{k}")
                    for n, w in enumerate((WQ, WK)):
                        terms = []
                        for j in range(C):
                            tile = slice(k * P, (k + 1) * P)
                            hi, lo = (xT[:, j, :, :].rearrange("p g n -> p (g n)") for xT in (xT_hi, xT_lo))
                            terms += [(w_hi[:, w, j, tile], hi), (w_hi[:, w, j, tile], lo), (w_lo[:, w, j, tile], hi)]
                        mm = split_product(bank[:, n * PAIR * P:(n + 1) * PAIR * P], terms)
                    mm.then_inc(qk_made, 1)

                def out_projection(g):
                    pe.wait_ge(clo_set, 2 * pb + g + 1)
                    if static == NP and pb == 0:
                        pe.wait_ge(w_split, 6)
                    ring_wait(pe, f"out{g}", t, static)
                    rows_by_weight(f"out{g}", lambda k: ctxT_hi[:, g, k, :], lambda k: ctxT_lo[:, g, k, :], WF)\
                        .then_inc(out_made, 1)

                def transpose_x1(g):
                    pe.wait_ge(x1_set, 2 * pb + g + 1)
                    ring_wait(pe, f"x1T{g}", t, static)
                    for k in range(C):
                        mm = pe.transpose(ring_bank(f"x1T{g}")[:, k * P:(k + 1) * P], x1[:, g, k * P:(k + 1) * P], idf[:])
                    mm.then_inc(x1T_made, 1)

                def value(g):
                    if static == NP and pa == 0:
                        pe.wait_ge(w_split, 3)
                    ring_wait(pe, f"v{g}", t, static)
                    rows_by_weight(f"v{g}", lambda k: xT_hi[:, k, g, :], lambda k: xT_lo[:, k, g, :], WV)\
                        .then_inc(v_made, 1)

                def project_value_bias():
                    pe.wait_ge(w_split, 4)
                    for k in range(C):
                        for part in (w_hi, w_lo):
                            mm = pe.matmul(logit[0][:, 0:D], cols[:, 2, k:k + 1].to_broadcast([P, P]),
                                           part[:, WF, k, :].bitcast(F32), start=(k == 0 and part is w_hi),
                                           stop=(k == C - 1 and part is w_lo))
                    mm.then_inc(bv_made, 1)

                def hidden(g):
                    pe.wait_ge(x1lo_set, 2 * pb + g + 1)
                    ring_wait(pe, f"h{g}", t, static)
                    rows_by_weight(f"h{g}", lambda k: x1T_hi[:, g, k, :], lambda k: x1T_lo[:, g, k, :], WH)\
                        .then_inc(h_made, 1)

                def gate_logit(g):
                    ring_wait(pe, f"g{g}", t, static)
                    rows_by_weight(f"g{g}", lambda k: x1T_hi[:, g, k, :], lambda k: x1T_lo[:, g, k, :], WG)\
                        .then_inc(g_made, 1)

                def scores(g, half):
                    if (g, half) == (0, 0):
                        if static == NP and pa == 0:
                            pe.wait_ge(const_in, 16 * N_CONST)
                        pe.wait_ge(maska_set, pa + 1)
                        pe.wait_ge(q_set, 3 * pa + 3)
                        pe.wait_ge(k_set, 3 * pa + 3)
                    ring_wait(pe, f"s{g}{half}", t, static)
                    bank = ring_bank(f"s{g}{half}")[:, 0:G0 * P]
                    pe.matmul(bank.rearrange("p (h m) -> p h m", h=G0), idh[:],
                              mask_a[:, g:g + 1, :].to_broadcast([P, G0, P]), start=True, stop=False,
                              skip_group_check=True)
                    feats = slice(half * DH0, (half + 1) * DH0)
                    for k in range(G0):
                        mm = pe.matmul(bank[:, k * P:(k + 1) * P], qT[feats, k, g, :], kT[feats, k, g, :],
                                       start=False, stop=(k == G0 - 1), skip_group_check=True)
                    mm.then_inc(s_made, 1)

                def transpose_probs(g, half):
                    pe.wait_ge(norm_set, 4 * pa + 2 * g + half + 1)
                    ring_wait(pe, f"pT{g}{half}", t, static)
                    for k in range(G0):
                        mm = pe.transpose(ring_bank(f"pT{g}{half}")[:, k * P:(k + 1) * P], prob[:, g, half * G0 + k, :],
                                          idf[:])
                    mm.then_inc(pT_made, 1)

                def transpose_parts():
                    pe.wait_ge(part_set, 3 * pb + 3)
                    ring_wait(pe, "termsT", t, static)
                    pe.transpose(ring_bank("termsT")[0:ROWS, 0:P // 2].bitcast(BF16),
                                 parts[:].rearrange("p c a h -> p (c a h)"), idh[:]).then_inc(termsT_made, 1)

                def mask_logits(j):
                    if j == 0:
                        pe.wait_ge(maskb_set, pb + 1)
                        if static == NP and pb == 0:
                            pe.wait_ge(bf_set, 1)
                    logit_wait(pe, "z", 0, j, t, static)
                    pe.matmul(logit_bank("z", 0, j)[:].rearrange("p (h m) -> p h m", h=G1), idh[:],
                              mask_b[:, 0:1, :].to_broadcast([P, G1, P]), start=True, stop=False, skip_group_check=True)

                def logits(g, j):
                    if (g, j) == (0, 0):
                        pe.wait_ge(termsT_set, pb + 1)
                    if g == 1:
                        logit_wait(pe, "z", g, j, t, static)
                    flat = logit_bank("z", g, j)[:]
                    if g == 0:
                        pe.matmul(flat, termsT[:], picks[:, 1, G1 * j:G1 * j + G1, :].rearrange("p h m -> p (h m)"),
                                  start=False, stop=False, skip_group_check=True)
                    for k in range(G1):
                        mm = pe.matmul(flat[:, k * P:(k + 1) * P], picks[:, 2 * g, G1 * j + k, :], termsT[:],
                                       start=(g == 1), stop=(k == G1 - 1), skip_group_check=True)
                    mm.then_inc(z_made, 1)

                def transpose_attention(g):
                    for j in range(NZ):
                        pe.wait_ge(att_set, 6 * pc + 3 * g + j + 1)
                        logit_wait(pe, "aT", g, j, t, static)
                        for k in range(G1):
                            mm = pe.transpose(logit_bank("aT", g, j)[:, k * P:(k + 1) * P], att[:, g, G1 * j + k, :], idf[:])
                        mm.then_inc(aT_made, 1)

                def aggregate(g):
                    ring_wait(pe, f"agg{g}", t, static)
                    bank = ring_bank(f"agg{g}")
                    for n in range(HEADS1):
                        j, k = divmod(n, G1)
                        if k == 0:
                            pe.wait_ge(aT_set, 6 * pc + 3 * g + j + 1)
                        mm = pe.matmul(bank[DH1 * k:DH1 * (k + 1), j * P:(j + 1) * P], h[:, g, n * DH1:(n + 1) * DH1],
                                       attT[:, g, n, :], start=True, stop=True)
                    mm.then_inc(agg_made, 1)

                def transpose_sums(g):
                    pe.wait_ge(aggT_set, 2 * pc + g + 1)
                    ring_wait(pe, f"f{g}", t, static)
                    for j in range(C):
                        mm = pe.transpose(ring_bank(f"f{g}")[:, j * P:(j + 1) * P], aggT[:, g, j, :], idf[:])
                    mm.then_inc(f_made, 1)

                if a:
                    qk(0)
                if b:
                    context(0)
                    context(1)
                if a:
                    qk(1)
                if b:
                    out_projection(0)
                    out_projection(1)
                if c:
                    transpose_attention(0)
                if a:
                    qk(2)
                if b:
                    transpose_x1(0)
                    transpose_x1(1)
                if c:
                    aggregate(0)
                if a:
                    scores(0, 0)
                    scores(0, 1)
                if static == NP and t == 0:
                    project_value_bias()
                if b:
                    hidden(0)
                if c:
                    transpose_sums(0)
                    transpose_attention(1)
                if b:
                    gate_logit(0)
                if c:
                    aggregate(1)
                if b:
                    hidden(1)
                if a:
                    scores(1, 0)
                    scores(1, 1)
                if c:
                    transpose_sums(1)
                if a:
                    value(0)
                    transpose_probs(0, 0)
                if b:
                    mask_logits(0)
                if a:
                    transpose_probs(0, 1)
                    value(1)
                if b:
                    transpose_parts()
                    mask_logits(1)
                    mask_logits(2)
                    logits(0, 0)
                    logits(0, 1)
                    logits(0, 2)
                if a:
                    transpose_probs(1, 0)
                    transpose_probs(1, 1)
                if b:
                    logits(1, 0)
                    logits(1, 1)
                    gate_logit(1)
                    logits(1, 2)

            run_ticks(pe, tick)

        @block.scalar
        def _(act):
            def round_weight(n):
                act.wait_ge(w_in[n], 16)
                act.activation(w_hi[:, n, :, :], raw_weight[n], ACT.Copy).then_inc(w_rounded, 1)

            def tick(t, static, a, b, c, d):
                pa, pb, pc, pd = t, t - 1, t - 2, t - 3

                def round_context(g):
                    act.wait_ge(ctx_made, 2 * pb + g + 1)
                    act.activation(ctxT_hi[:, g, :, :].rearrange("p c n -> p (c n)"), ring_bank(f"ctx{g}")[:, 0:D],
                                   ACT.Copy).then_inc(chi_set, 1)

                def query(k):
                    act.wait_ge(qk_made, 3 * pa + k + 1)
                    act.activation(qT[:, k, :, :].rearrange("p g n -> p (g n)"), ring_bank(f"qk{k}")[:, 0:PAIR * P],
                                   ACT.Identity, bias=cols[:, 0, k:k + 1], scale=Q_SCALE)\
                        .then_inc(q_set, 1)

                def attention_exp(g, j):
                    act.wait_ge(leaky_set, 6 * pc + 3 * g + j + 1)
                    for n in range(G1 * j, G1 * j + G1):
                        op = act.activation(att[:, g, n, :], att[:, g, n, :], ACT.Exp, scale=-1.0,
                                            bias=att_min[:, g, n:n + 1], accum_out=att_sum[:, g, n:n + 1])
                    op.then_inc(att_set, 1)

                def keep_attT(g):
                    for j in range(NZ):
                        act.wait_ge(aT_made, 6 * pc + 3 * g + j + 1)
                        act.activation(attT[:, g, G1 * j:G1 * j + G1, :].rearrange("p h n -> p (h n)"),
                                       logit_bank("aT", g, j)[:], ACT.Copy).then_inc(aT_set, 1)

                def keep_sums(g):
                    act.wait_ge(agg_made, 2 * pc + g + 1)
                    act.activation(aggT[:, g, :, :].rearrange("p c n -> p (c n)"), ring_bank(f"agg{g}")[:, 0:D],
                                   ACT.Copy).then_inc(aggT_set, 1)

                def keep_probT(g, half):
                    act.wait_ge(pT_made, 4 * pa + 2 * g + half + 1)
                    act.activation(probT[:, g, half * G0:(half + 1) * G0, :].rearrange("p h n -> p (h n)"),
                                   ring_bank(f"pT{g}{half}")[:, 0:G0 * P], ACT.Copy).then_inc(pT_set, 1)

                def keep_value(g):
                    act.wait_ge(v_made, 2 * pa + g + 1)
                    act.activation(v[:, g, :], ring_bank(f"v{g}")[:, 0:D], ACT.Copy).then_inc(v_set, 1)

                def round_x1(g):
                    act.wait_ge(x1T_made, 2 * pb + g + 1)
                    act.activation(x1T_hi[:, g, :, :].rearrange("p c n -> p (c n)"), ring_bank(f"x1T{g}")[:, 0:D],
                                   ACT.Copy).then_inc(x1hi_set, 1)

                def elu_exp(g):
                    act.wait_ge(fneg_set, 2 * pc + g + 1)
                    act.activation(gated[:, g, :], gated[:, g, :], ACT.Exp).then_inc(fexp_set, 1)

                def tanh_hidden(g):
                    act.wait_ge(h_made, 2 * pb + g + 1)
                    act.activation(th[:, g, :], ring_bank(f"h{g}")[:, 0:D], ACT.Tanh).then_inc(th_set, 1)

                def tanh_gate(g, pair):
                    act.wait_ge(gpre_set, 2 * pair + g + 1)
                    act.activation(g_tanh[:, g, :], g_tanh[:, g, :], ACT.Tanh, scale=0.5).then_inc(gtanh_set, 1)

                def score_exp(g, half):
                    act.wait_ge(max_set, 4 * pa + 2 * g + half + 1)
                    for k in range(G0):
                        n = half * G0 + k
                        op = act.activation(prob[:, g, n, :], ring_bank(f"s{g}{half}")[:, k * P:(k + 1) * P], ACT.Exp,
                                            bias=neg_max[:, g, n:n + 1], accum_out=p_sum[:, g, n:n + 1])
                    op.then_inc(prob_set, 1)

                def relu_logits(g, j):
                    act.wait_ge(z_made, 6 * pb + 3 * g + j + 1)
                    if g == 0:
                        act.activation(att[:, g, G1 * j:G1 * j + G1, :].rearrange("p h m -> p (h m)"),
                                       logit_bank("z", g, j)[:], ACT.Relu, scale=1.0 / SLOPE - 1.0).then_inc(relu_set[g], 1)
                        return
                    if j == 0:
                        act.wait_ge(source_set, pb + 1)
                    for n in range(G1 * j, G1 * j + G1):
                        op = act.activation(att[:, g, n, :], logit_bank("z", g, j)[:, (n - G1 * j) * P:(n - G1 * j + 1) * P],
                                            ACT.Relu, bias=source[:, n:n + 1], scale=1.0 / SLOPE - 1.0)
                    op.then_inc(relu_set[g], 1)

                if c:
                    attention_exp(0, 0)
                if a:
                    query(0)
                if b:
                    round_context(0)
                    round_context(1)
                if c:
                    attention_exp(0, 1)
                    tanh_gate(1, pc)
                if a:
                    query(1)
                if c:
                    attention_exp(0, 2)
                    attention_exp(1, 0)
                    keep_attT(0)
                    attention_exp(1, 1)
                if static == NP and t == 0:
                    for n in range(WV, WG + 1):
                        round_weight(n)
                if b:
                    round_x1(0)
                    round_x1(1)
                if c:
                    attention_exp(1, 2)
                    keep_sums(0)
                if a:
                    score_exp(0, 0)
                if b:
                    tanh_hidden(0)
                if a:
                    score_exp(0, 1)
                if c:
                    keep_attT(1)
                    elu_exp(0)
                    keep_sums(1)
                if b:
                    tanh_gate(0, pb)
                    tanh_hidden(1)
                if a:
                    score_exp(1, 0)
                    score_exp(1, 1)
                    keep_value(0)
                if c:
                    elu_exp(1)
                if a:
                    keep_probT(0, 0)
                    keep_probT(0, 1)
                    keep_value(1)
                if b:
                    for j in range(NZ):
                        relu_logits(0, j)
                if a:
                    keep_probT(1, 0)
                    keep_probT(1, 1)
                if b:
                    for j in range(NZ):
                        relu_logits(1, j)

            round_weight(WQ)
            round_weight(WK)
            act.wait_ge(bq_scaled, 1)
            run_ticks(act, tick)

        @block.vector
        def _(dve):
            def round_x(g, pair):
                if g == 0:
                    dve.wait_ge(xT_loaded, 16 * pair + 16)
                dve.tensor_copy(xT_hi[:, :, g, :], xT_in[:, :, g, :]).then_inc(xhi_set, 1)

            def carried_wait(s, value):
                dve.wait_ge(bq_scaled, 1)
                dve.wait_ge(s, value)

            round_x(0, 0)
            round_x(1, 0)
            def rest_weight(n):
                dve.wait_ge(w_rounded, n + 1)
                dve.tensor_tensor(w_lo[:, n, :, :], raw_weight[n], w_hi[:, n, :, :].bitcast(F32),
                                  ALU.subtract).then_inc(w_split, 1)

            rest_weight(WQ)
            rest_weight(WK)
            dve.wait_ge(cols_in, 16)
            dve.tensor_scalar(cols[:, 0, :], cols[:, 0, :], Q_SCALE, None, ALU.mult).then_inc(bq_scaled, 1)

            def tick(t, static, a, b, c, d):
                pa, pb, pc, pd = t, t - 1, t - 2, t - 3

                def keep_mask():
                    if static is None or pb > 0:
                        dve.wait_ge(z_made, 6 * pb)
                        dve.wait_ge(masked_set, NZ * pb)
                    dve.wait_ge(maska_set, pb + 1)
                    dve.tensor_copy(mask_b[:], mask_a[:]).then_inc(maskb_set, 1)

                def make_mask():
                    dve.wait_ge(adj_loaded, 16 * pa + 16)
                    if static is None or pa > 0:
                        dve.wait_ge(s_made, 4 * pa)
                        dve.wait_ge(maskb_set, pa)
                    dve.tensor_scalar(mask_a[:], adj_in[:], -1.0, -MASKED, ALU.add, ALU.mult).then_inc(maska_set, 1)

                def rest_context(g):
                    dve.wait_ge(chi_set, 2 * pb + g + 1)
                    dve.tensor_tensor(ctxT_lo[:, g, :, :].rearrange("p c n -> p (c n)"), ring_bank(f"ctx{g}")[:, 0:D],
                                      ctxT_hi[:, g, :, :].rearrange("p c n -> p (c n)").bitcast(F32), ALU.subtract)\
                       .then_inc(clo_set, 1)

                def query(k):
                    dve.wait_ge(qk_made, C * pa + k + 1)
                    dve.tensor_scalar(qT[:, k, :, :].rearrange("p g n -> p (g n)"), ring_bank(f"qk{k}")[:, 0:PAIR * P],
                                      Q_SCALE, cols[:, 0, k:k + 1], ALU.mult, ALU.add).then_inc(q_set, 1)

                def key(k):
                    dve.wait_ge(q_set, C * pa + k + 1)
                    dve.tensor_scalar(kT[:, k, :, :].rearrange("p g n -> p (g n)"),
                                      ring_bank(f"qk{k}")[:, PAIR * P:2 * PAIR * P],
                                      cols[:, 1, k:k + 1], None, ALU.add).then_inc(k_set, 1)

                def residual(g):
                    dve.wait_ge(out_made, 2 * pb + g + 1)
                    dve.wait_ge(xres_set, 2 * pb + g + 1)
                    dve.tensor_tensor(x1[:, g, :], ring_bank(f"out{g}")[:, 0:D], x_res[:, g, :], ALU.add).then_inc(y0_set, 1)
                    dve.wait_ge(y0_set, 2 * pb + g + 1)
                    dve.bn_stats(stats0[:, g, :], x1[:, g, :]).then_inc(st0_set, 1)

                def aggregate0(g):
                    carried_wait(st0_set, 2 * pb + g + 1)
                    dve.bn_aggr(mv0[:, g, :], stats0[:, g, :]).then_inc(mv0_set, 1)

                def normalize0(g):
                    dve.wait_ge(rstd0_set, 2 * pb + g + 1)
                    dve.tensor_scalar(x1[:, g, :], x1[:, g, :], mv0[:, g, 0:1], rstd0[:, g:g + 1], ALU.subtract, ALU.mult)\
                       .then_inc(x1_set, 1)

                def rest_x1(g):
                    dve.wait_ge(x1hi_set, 2 * pb + g + 1)
                    dve.tensor_tensor(x1T_lo[:, g, :, :].rearrange("p c n -> p (c n)"), ring_bank(f"x1T{g}")[:, 0:D],
                                      x1T_hi[:, g, :, :].rearrange("p c n -> p (c n)").bitcast(F32), ALU.subtract)\
                       .then_inc(x1lo_set, 1)

                def hidden(g):
                    dve.wait_ge(th_set, 2 * pb + g + 1)
                    if static is None or pb > 0:
                        dve.wait_ge(agg_made, 2 * (pb - 1) + g + 1)
                    dve.tensor_tensor(h[:, g, :], ring_bank(f"h{g}")[:, 0:D], rows[:, BH, :], ALU.add).then_inc(h_set, 1)

                def add_value_bias():
                    dve.wait_ge(const_in, 16 * N_CONST)
                    dve.wait_ge(bv_made, 1)
                    dve.tensor_tensor(rows[:, BF, :], logit[0][:, 0:D], rows[:, BF, :], ALU.add).then_inc(bf_set, 1)

                def gate_bias(g):
                    dve.wait_ge(g_made, 2 * pb + g + 1)
                    dve.tensor_tensor(g_tanh[:, g, :], ring_bank(f"g{g}")[:, 0:D], rows[:, BG, :], ALU.add).then_inc(gpre_set, 1)

                def score_max(g, half):
                    dve.wait_ge(s_made, 4 * pa + 2 * g + half + 1)
                    dve.tensor_reduce(neg_max[:, g, half * G0:(half + 1) * G0],
                                      ring_bank(f"s{g}{half}")[:, 0:G0 * P].rearrange("p (h m) -> p h m", h=G0),
                                      AX.X, ALU.max, negate=True).then_inc(max_set, 1)

                def invert_sum(g, half):
                    dve.wait_ge(prob_set, 4 * pa + 2 * g + half + 1)
                    heads = slice(half * G0, (half + 1) * G0)
                    dve.reciprocal(p_inv[:, g, heads], p_sum[:, g, heads]).then_inc(inv_set, 1)

                def logit_terms(g):
                    dve.wait_ge(thw_set, 2 * pb + g + 1)
                    dve.tensor_reduce(terms[:, g, :, :].rearrange("p s h -> p (s h)"),
                                      th_w[:, g, :, :].rearrange("p s (h e) -> p (s h) e", e=DH1),
                                      AX.X, ALU.add).then_inc(terms_set, 1)

                def split_terms():
                    added = terms[:].rearrange("p g s h -> p (g s) h")[:, 0:KINDS, :]
                    dve.wait_ge(terms_set, 2 * pb + 2)
                    dve.tensor_copy(parts[:, :, 0, :], added).then_inc(part_set, 1)
                    dve.wait_ge(part_set, 3 * pb + 1)
                    dve.tensor_tensor(rest[:], added, parts[:, :, 0, :], ALU.subtract).then_inc(rest_set, 1)
                    dve.wait_ge(rest_set, 2 * pb + 1)
                    dve.tensor_copy(parts[:, :, 1, :], rest[:]).then_inc(part_set, 1)
                    dve.wait_ge(part_set, 3 * pb + 2)
                    dve.tensor_tensor(rest2[:], rest[:], parts[:, :, 1, :], ALU.subtract).then_inc(rest_set, 1)
                    dve.wait_ge(rest_set, 2 * pb + 2)
                    dve.tensor_copy(parts[:, :, 2, :], rest2[:]).then_inc(part_set, 1)
                    dve.tensor_scalar(source[:], terms[:, 1, 1, :], 1.0 / SLOPE - 1.0, None, ALU.mult).then_inc(source_set, 1)

                def keep_terms():
                    dve.wait_ge(termsT_made, pb + 1)
                    dve.tensor_copy(termsT[:], ring_bank("termsT")[0:ROWS, 0:P // 2].bitcast(BF16)).then_inc(termsT_set, 1)

                def leaky(g, j):
                    carried_wait(relu_set[0] if g == 0 else masked_set, NZ * pb + j + 1 if j < NZ - 1 else NZ * pa)
                    for n in range(G1 * j, G1 * j + G1):
                        op = dve.tensor_tensor_reduce(
                            out=att[:, g, n, :], in0=logit_bank("z", g, j)[:, (n - G1 * j) * P:(n - G1 * j + 1) * P],
                            in1=att[:, g, n, :], scale=-SLOPE, scalar=3.0e38, op0=ALU.add, op1=ALU.min,
                            accum_out=att_min[:, g, n:n + 1])
                    op.then_inc(leaky_set, 1)

                def weigh(g):
                    dve.wait_ge(att_set, 6 * pc + 3 * g + 3)
                    dve.reciprocal(a_inv[:, g, :], att_sum[:, g, :]).then_inc(ainv_set, 1)
                    dve.wait_ge(ainv_set, 2 * pc + g + 1)
                    dve.wait_ge(f_made, 2 * pc + g + 1)
                    dve.tensor_tensor(f[:, g, :].rearrange("p (h e) -> p h e", h=HEADS1),
                                      ring_bank(f"f{g}")[:, 0:D].rearrange("p (h e) -> p h e", h=HEADS1),
                                      a_inv[:, g, :].unsqueeze(2).to_broadcast([P, HEADS1, DH1]), ALU.mult).then_inc(f_set, 1)
                    dve.wait_ge(f_set, 2 * pc + g + 1)
                    dve.tensor_scalar(gated[:, g, :], f[:, g, :], 0.0, None, ALU.min).then_inc(fneg_set, 1)

                def elu_and_gate(g):
                    dve.wait_ge(fexp_set, 2 * pc + g + 1)
                    dve.scalar_tensor_tensor(out=gated[:, g, :], in0=f[:, g, :], scalar=0.0, in1=gated[:, g, :],
                                             op0=ALU.max, op1=ALU.add).then_inc(elu_set, 1)
                    dve.wait_ge(elu_set, 2 * pc + g + 1)
                    dve.wait_ge(gate_set, 2 * pc + g + 1)
                    dve.scalar_tensor_tensor(out=gated[:, g, :], in0=gated[:, g, :], scalar=-1.0, in1=gate[:, g, :],
                                             op0=ALU.add, op1=ALU.mult).then_inc(gated_set, 1)

                def ungated(g, pair):
                    dve.wait_ge(gate_set, 2 * pair + g + 1)
                    if static is None or pair > 0:
                        dve.wait_ge(y1_set, 2 * (pair - 1) + g + 1)
                    dve.scalar_tensor_tensor(out=gx[:, g, :], in0=gate[:, g, :], scalar=-2.0, in1=x1[:, g, :],
                                             op0=ALU.add, op1=ALU.mult).then_inc(gx_set, 1)

                def moments1(g):
                    dve.wait_ge(y1_set, 2 * pd + g + 1)
                    dve.bn_stats(stats1[:, g, :], y1[:, g, :]).then_inc(st1_set, 1)

                def aggregate1(g):
                    carried_wait(st1_set, 2 * pd + g + 1)
                    dve.bn_aggr(mv1[:, g, :], stats1[:, g, :]).then_inc(mv1_set, 1)

                def normalize1(g):
                    if g == 0 and (static is None or pd > 0):
                        dve.wait_ge(stored, 16 * pd)
                    dve.wait_ge(rstd1_set, 2 * pd + g + 1)
                    dve.tensor_scalar(y_out[:, g, :], y1[:, g, :], mv1[:, g, 0:1], rstd1[:, g:g + 1], ALU.subtract, ALU.mult)\
                       .then_inc(yout_set, 1)

                if a:
                    key(0)
                if b:
                    rest_context(0)
                    rest_context(1)
                    keep_mask()
                if a:
                    make_mask()
                    key(1)
                if c:
                    ungated(1, pc)
                if b:
                    residual(0)
                    aggregate0(0)
                    residual(1)
                    aggregate0(1)
                    normalize0(0)
                    normalize0(1)
                if a:
                    query(2)
                    key(2)
                if b:
                    rest_x1(0)
                    rest_x1(1)
                if d:
                    moments1(0)
                if a:
                    score_max(0, 0)
                if d:
                    moments1(1)
                if a:
                    score_max(0, 1)
                if static == NP and t == 0:
                    for n in range(WV, WG + 1):
                        rest_weight(n)
                    add_value_bias()
                if d:
                    aggregate1(0)
                    aggregate1(1)
                if b:
                    hidden(0)
                if c:
                    weigh(0)
                if a:
                    invert_sum(0, 0)
                    invert_sum(0, 1)
                if d:
                    normalize1(0)
                    normalize1(1)
                if b:
                    gate_bias(0)
                if c:
                    elu_and_gate(0)
                if b:
                    logit_terms(0)
                    hidden(1)
                if a:
                    score_max(1, 0)
                    score_max(1, 1)
                if c:
                    weigh(1)
                if b:
                    logit_terms(1)
                    split_terms()
                if a:
                    invert_sum(1, 0)
                    invert_sum(1, 1)
                if b:
                    keep_terms()
                if static is None or t + 1 < NP:
                    dve.wait_ge(v_made, 2 * t + 2)
                    round_x(0, t + 1)
                    round_x(1, t + 1)
                if b:
                    leaky(0, 0)
                    leaky(0, 1)
                if c:
                    elu_and_gate(1)
                if b:
                    leaky(0, 2)
                    ungated(0, pb)
                    leaky(1, 0)
                    gate_bias(1)
                    leaky(1, 1)
                    leaky(1, 2)

            run_ticks(dve, tick)

        @block.gpsimd
        def _(pool):
            def rest_x(g, pair):
                pool.wait_ge(xhi_set, 2 * pair + g + 1)
                pool.tensor_tensor(xT_lo[:, :, g, :], xT_in[:, :, g, :], xT_hi[:, :, g, :].bitcast(F32),
                                   ALU.subtract).then_inc(xlo_set, 1)

            def tick(t, static, a, b, c, d):
                pa, pb, pc, pd = t, t - 1, t - 2, t - 3

                def residual_input(g):
                    if g == 0 and static == NP and pa == 0:
                        pool.wait_ge(bf_set, 1)
                    if g == 0:
                        pool.wait_ge(x_loaded, 16 * pa + 16)
                    if static is None or pa > 0:
                        pool.wait_ge(y0_set, 2 * (pa - 1) + g + 1)
                    pool.tensor_tensor(x_res[:, g, :], x_in[:, g, :], rows[:, BF, :], ALU.add).then_inc(xres_set, 1)

                def inverse_deviation(g, mv, ve, rstd, mv_set, ve_set, rstd_set, pair):
                    pool.wait_ge(mv_set, 2 * pair + g + 1)
                    pool.tensor_tensor(ve[:, g:g + 1], mv[:, g, 1:2], eps[:], ALU.add).then_inc(ve_set, 1)
                    pool.wait_ge(ve_set, 2 * pair + g + 1)
                    pool.tensor_tensor(rstd[:, g:g + 1], ve[:, g:g + 1], neg_half[:], ALU.pow).then_inc(rstd_set, 1)

                def gated_sum(g):
                    pool.wait_ge(gated_set, 2 * pc + g + 1)
                    pool.wait_ge(gx_set, 2 * pc + g + 1)
                    pool.tensor_tensor(y1[:, g, :], gated[:, g, :], gx[:, g, :], ALU.subtract).then_inc(y1_set, 1)

                def normalize_probs(g, half):
                    pool.wait_ge(inv_set, 4 * pa + 2 * g + half + 1)
                    heads = slice(half * G0, (half + 1) * G0)
                    pool.tensor_tensor(prob[:, g, heads, :], prob[:, g, heads, :],
                                       p_inv[:, g, heads].unsqueeze(2).to_broadcast([P, G0, P]), ALU.mult).then_inc(norm_set, 1)

                def mask_logits(j):
                    pool.wait_ge(relu_set[1], NZ * pb + j + 1)
                    heads = slice(G1 * j, G1 * j + G1)
                    pool.tensor_tensor(att[:, 1, heads, :], att[:, 1, heads, :],
                                       mask_b[:, 1:2, :].to_broadcast([P, G1, P]), ALU.add).then_inc(masked_set, 1)

                def gate_value(g):
                    pool.wait_ge(half_set, 2)
                    pool.wait_ge(gtanh_set, 2 * pb + g + 1)
                    if static is None or pb > 0:
                        pool.wait_ge(gated_set, 2 * pc + g + 1)
                    pool.tensor_scalar(gate[:, g, :], g_tanh[:, g, :], 0.5, 0.5, ALU.mult, ALU.add).then_inc(gate_set, 1)

                def weigh_hidden(g):
                    pool.wait_ge(th_set, 2 * pb + g + 1)
                    pool.tensor_tensor(th_w[:, g, :, :], th[:, g:g + 1, :].to_broadcast([P, 2, D]),
                                       rows[:, W_DST:W_SRC + 1, :], ALU.mult).then_inc(thw_set, 1)

                if b:
                    inverse_deviation(0, mv0, ve0, rstd0, mv0_set, ve0_set, rstd0_set, pb)
                    inverse_deviation(1, mv0, ve0, rstd0, mv0_set, ve0_set, rstd0_set, pb)
                if a:
                    residual_input(0)
                    residual_input(1)
                if d:
                    inverse_deviation(0, mv1, ve1, rstd1, mv1_set, ve1_set, rstd1_set, pd)
                    inverse_deviation(1, mv1, ve1, rstd1, mv1_set, ve1_set, rstd1_set, pd)
                if b:
                    weigh_hidden(0)
                if a:
                    normalize_probs(0, 0)
                    normalize_probs(0, 1)
                if c:
                    gated_sum(0)
                if b:
                    weigh_hidden(1)
                if a:
                    normalize_probs(1, 0)
                    normalize_probs(1, 1)
                if b:
                    gate_value(0)
                if static is None or t + 1 < NP:
                    rest_x(0, t + 1)
                    rest_x(1, t + 1)
                if b:
                    for j in range(NZ):
                        mask_logits(j)
                if c:
                    gated_sum(1)
                if b:
                    gate_value(1)

            pool.memset(neg_half[:], -0.5).then_inc(half_set, 1)
            pool.memset(eps[:], EPS).then_inc(half_set, 1)
            pool.wait_ge(half_set, 2)
            rest_x(0, 0)
            rest_x(1, 0)
            run_ticks(pool, tick)


def kernel(**inputs):
    import concourse.bacc as bacc
    import ml_dtypes
    import numpy as np
    from concourse.bass_utils import run_bass_kernel_spmd

    def arr(name):
        return np.asarray(inputs[name])

    def by_partition(w):
        return w.reshape(-1, P, w.shape[-1]).transpose(1, 0, 2)

    x, adj = arr("x"), arr("adj")
    D = x.shape[-1]
    W, w_src, w_dst = arr("L1_gnn_W"), arr("L1_gnn_w_src"), arr("L1_gnn_w_dst")
    heads = W.shape[0]
    row, kinds = np.arange(3 * PARTS * heads)[:, None, None], np.arange(3)[:, None]
    pick = (row % heads == np.arange(heads)) & (row // (PARTS * heads) == kinds)
    pick = pick[:, :, :, None] & np.ones(P, bool)
    arrays = {
        "x": x,
        "xT": x.reshape(-1, PAIR, P, D // P, P).transpose(0, 4, 3, 1, 2),
        "adj": adj.transpose(1, 0, 2),
        "weights": np.stack([by_partition(w) for w in (
            arr("L0_gnn_Wq"), arr("L0_gnn_Wk"), arr("L0_gnn_Wv"), arr("L0_gnn_Wf"),
            W.transpose(1, 0, 2).reshape(D, -1), arr("L1_gnn_H_w").T)]),
        "bias_rows": np.stack([np.broadcast_to(b, (P, D)) for b in (
            arr("L0_gnn_bf"), np.tile(arr("L1_gnn_b"), heads), arr("L1_gnn_H_b"),
            w_dst.reshape(D), w_src.reshape(D))], axis=1),
        "bias_cols": np.stack([arr(n).reshape(-1, P).T for n in ("L0_gnn_bq", "L0_gnn_bk", "L0_gnn_bv")], axis=1),
        "ident": np.eye(P, dtype=np.float32),
        "ident_h": np.eye(P, dtype=ml_dtypes.bfloat16),
        "pick": pick.astype(ml_dtypes.bfloat16),
    }
    arrays = {n: np.ascontiguousarray(a) for n, a in arrays.items()}
    nc = bacc.Bacc("TRN2", target_bir_lowering=False, num_devices=1)
    args = [nc.dram_tensor(n, a.shape, mybir.dt.from_np(a.dtype), kind="ExternalInput").ap() for n, a in arrays.items()]
    out = nc.dram_tensor("out", x.shape, F32, kind="ExternalOutput").ap()
    build(nc, *args, out)
    result = run_bass_kernel_spmd(nc, [arrays], core_ids=[0])
    return result.results[0]["out"]
```
